# Optimizing a Trainium2 kernel written in Bass

```python
import numpy as np
import jax
import jax.numpy as jnp

def _softmax(x, axis=-1):
    return jax.nn.softmax(x, axis=axis)

def _gelu(x):
    return jax.nn.gelu(x, approximate=True)

def _silu(x):
    return jax.nn.silu(x)

def _sigmoid(x):
    return jax.nn.sigmoid(x)

def _layernorm(x, axis=-1, eps=1e-05):
    m = jnp.mean(x, axis=axis, keepdims=True)
    v = jnp.var(x, axis=axis, keepdims=True)
    return (x - m) / jnp.sqrt(v + eps)

def _scatter_add(tgt, idx, src, axis=0):
    return tgt.at[idx].add(src)

def _segment_sum(src, seg, n):
    return jax.ops.segment_sum(src, seg, n)
kernel_name = 'mk_adj_preln_d2_adj_r2_6bac71'

def setup_inputs(seed: int=0):
    np.random.seed(seed)
    _w = jnp.asarray

    def _rec_inputs():
        import jax
        import jax.numpy as jnp
        _gk = jax.random.key(seed)
        x = -0.000929 + 1 * jax.random.normal(jax.random.fold_in(_gk, 1), (8192, 128), jnp.float32)
        _a = jax.random.bernoulli(jax.random.fold_in(_gk, 2), 0.000976562, (8192, 8192))
        adj = _a.astype(jnp.int32)
        return (x, adj)
    x, adj = _rec_inputs()

    def _L0_gnn_setup():
        import jax, jax.numpy as jnp
        import numpy as np
        N = 4096
        IN_F = 128
        OUT_F = 128
        ALPHA = 0.2
        NEG_INF = -9000000000000000.0
        key = jax.random.key(seed)
        k1, k2, k3, k4 = jax.random.split(key, 4)
        h = jax.random.normal(k1, (N, IN_F), dtype=jnp.float32)
        adj = jax.random.randint(k2, (N, N), 0, 2, dtype=jnp.int32)
        W = jax.random.normal(k3, (IN_F, OUT_F), dtype=jnp.float32) * (1.0 / np.sqrt(IN_F))
        limit = 1.414 * np.sqrt(6.0 / (2 * OUT_F + 1))
        a = jax.random.uniform(k4, (2 * OUT_F, 1), dtype=jnp.float32, minval=-limit, maxval=limit)
        return {'h': h, 'adj': adj, 'W': W, 'a': a}
    _L0_gnn_all = _L0_gnn_setup()
    _L0_gnn_in = {k: v for k, v in _L0_gnn_all.items() if k in ('W', 'a')}
    del _L0_gnn_all

    def _L1_gnn_setup():
        import jax, jax.numpy as jnp
        import numpy as np
        ALPHA = 0.2
        NEG_INF = -9000000000000000.0
        key = jax.random.key(seed)
        k1, k2, k3, k4 = jax.random.split(key, 4)
        N, F_IN, F_OUT = (4096, 128, 128)
        h = jax.random.normal(k1, (N, F_IN), dtype=jnp.float32)
        adj = jax.random.randint(k2, (N, N), 0, 2, dtype=jnp.int32)
        W = jax.random.normal(k3, (F_IN, F_OUT), dtype=jnp.float32) * (1.414 / np.sqrt(F_IN))
        a = jax.random.normal(k4, (2 * F_OUT, 1), dtype=jnp.float32) * (1.414 / np.sqrt(2 * F_OUT))
        return {'h': h, 'adj': adj, 'W': W, 'a': a}
    _L1_gnn_all = _L1_gnn_setup()
    _L1_gnn_in = {k: v for k, v in _L1_gnn_all.items() if k in ('W', 'a')}
    del _L1_gnn_all
    return {'x': x, 'adj': adj, 'L0_gnn_W': _L0_gnn_in['W'], 'L0_gnn_a': _L0_gnn_in['a'], 'L1_gnn_W': _L1_gnn_in['W'], 'L1_gnn_a': _L1_gnn_in['a']}

def reference(x, adj, L0_gnn_W, L0_gnn_a, L1_gnn_W, L1_gnn_a):
    import jax
    import jax.numpy as jnp

    def _L0_gnn_ref(h, adj, W, a):
        import jax, jax.numpy as jnp
        import numpy as np
        N = 4096
        IN_F = 128
        OUT_F = 128
        ALPHA = 0.2
        NEG_INF = -9000000000000000.0
        Wh = h @ W
        a1 = a[:OUT_F, 0]
        a2 = a[OUT_F:, 0]
        s1 = Wh @ a1
        s2 = Wh @ a2
        e = jax.nn.leaky_relu(s1[:, None] + s2[None, :], negative_slope=ALPHA)
        masked = jnp.where(adj > 0, e, NEG_INF)
        attention = jax.nn.softmax(masked, axis=1)
        h_prime = attention @ Wh
        return jax.nn.elu(h_prime)

    def _L1_gnn_ref(h, adj, W, a):
        import jax, jax.numpy as jnp
        import numpy as np
        ALPHA = 0.2
        NEG_INF = -9000000000000000.0
        Wh = h @ W
        F_out = W.shape[1]
        e_src = Wh @ a[:F_out, 0]
        e_dst = Wh @ a[F_out:, 0]
        e = jax.nn.leaky_relu(e_src[:, None] + e_dst[None, :], negative_slope=ALPHA)
        attention = jax.nn.softmax(jnp.where(adj > 0, e, NEG_INF), axis=1)
        h_prime = attention @ Wh
        return h_prime
    h = jnp.maximum(_layernorm(x, axis=-1), 0.0)
    x = x + _L0_gnn_ref(h, adj, L0_gnn_W, L0_gnn_a)
    h = jnp.maximum(_layernorm(x, axis=-1), 0.0)
    x = x + _L1_gnn_ref(h, adj, L1_gnn_W, L1_gnn_a)
    return x

_drawn_inputs = setup_inputs


def setup_inputs(seed=0):
    import zlib

    import numpy as np

    out = dict(_drawn_inputs(seed))
    spreads = {}
    factors = {}
    for name, (base, spread) in spreads.items():
        noise = np.random.default_rng([zlib.crc32(name.encode()), seed]).standard_normal(out[name].shape)
        drawn = base * np.exp(spread * noise) if base else spread * noise
        out[name] = jnp.asarray(drawn.astype(out[name].dtype))
    for name, factor in factors.items():
        out[name] = (out[name] * factor).astype(out[name].dtype)
    return out
```

```python
from contextlib import ExitStack

import concourse.bass as bass
from concourse import mybir

ALU = mybir.AluOpType
ACT = mybir.ActivationFunctionType
AX_X = mybir.AxisListType.X
F32 = mybir.dt.float32
BF16 = mybir.dt.bfloat16
U8 = mybir.dt.uint8
I32 = mybir.dt.int32

P = 128
SLOPE = 0.2
EPS = 1e-5


def gat_two_layers(nc, x, adj, w0, a0, w1, a1, out):
    N, F = x.shape
    NT = N // P
    BT = 8
    BI = BT * P
    NB = NT // BT
    CT = 4
    CJ = CT * P
    BODY = 2 * CT
    NCC = NT // BODY
    GW = F + 1
    PER_BANK = 3
    BANKS = 3
    LEAD = 3
    PR = 4
    HR = BT // 2

    ctx = ExitStack()
    with ctx:
        def sb(name, shape, dt=F32):
            return ctx.enter_context(nc.sbuf_tensor(name, shape, dt))

        def sem(name):
            return ctx.enter_context(nc.semaphore(name))

        x_sb = sb("x_sb", [P, NT, F])
        g_sb = sb("g_sb", [P, NT, GW])
        q_sb = sb("q_sb", [P, N])
        adj_sb = sb("adj_sb", [P, 4, HR, CJ], I32)
        row_sb = sb("row_sb", [P, 2, BT, CJ], BF16)
        col_sb = sb("col_sb", [P, 2, CT, BI], U8)
        p_sb = sb("p_sb", [P, PR, BI])
        acc_sb = sb("acc_sb", [P, BANKS * PER_BANK, GW])
        t_sb = sb("t_sb", [P, NT])
        f_sb = sb("f_sb", [P, NT])
        hid = sb("hid", [P, 2, BT, F])
        sq = sb("sq", [P, BT, F])
        hT = sb("hT", [P, 2, BI])
        wa = sb("wa", [P, 2, GW])
        w_rep = sb("w_rep", [P, 2, P])
        w_T = sb("w_T", [P, 2, P])
        a_sb = sb("a_sb", [P, 2, 2])
        a_rep = sb("a_rep", [P, 2, P])
        ident = sb("ident", [P, P])
        ident16 = sb("ident16", [P, P], BF16)
        zeros16 = sb("zeros16", [P, PER_BANK * GW], BF16)
        ones = sb("ones", [P, P])
        st = sb("st", [P, 2, 4, BT])
        hsum = sb("hsum", [P, 2, NB])
        hs_rep = sb("hs_rep", [P, P])
        wh_mean = sb("wh_mean", [P, F])
        mx = sb("mx", [P, 4])
        den = sb("den", [P, 3, BT])
        hp, corr, ex = hid[:, 0], hid[:, 1], sq

        psum = ctx.enter_context(nc.psum_tensor("psum", [P, 8, 512], F32))
        ps_all = [psum[:, i, :] for i in range(8)]
        pt = [ps_all[3].bitcast(BF16), ps_all[4].bitcast(BF16)]

        mask_dram = nc.dram_tensor("mask_cols", [NB, NCC * 2, P, CT * BI], U8, kind="Internal").ap()
        acc_dram = nc.dram_tensor("acc_rows", [2, NB, P, BANKS * PER_BANK * GW], F32, kind="Internal").ap()

        def acc_tile(r):
            return ps_all[r // PER_BANK][:, (r % PER_BANK) * GW:(r % PER_BANK) * GW + GW]

        x_in = [sem(f"x_in{b}") for b in range(NB)]
        w_in = sem("w_in")
        const_ready = sem("const_ready")
        wprep_pe = sem("wprep_pe")
        wprep_sb = sem("wprep_sb")
        adj_in = [sem(f"adj_in{i}") for i in range(4)]
        converted = sem("converted")
        transposed = sem("transposed")
        evacuated = sem("evacuated")
        stored = [sem(f"stored{i}") for i in range(2)]
        mask_in = [sem(f"mask_in{i}") for i in range(2)]
        L = range(2)
        p_ready = [sem(f"p_ready{l}") for l in L]
        p_used = [sem(f"p_used{l}") for l in L]
        acc_saved = [sem(f"acc_saved{l}") for l in L]
        acc_out = [sem(f"acc_out{l}") for l in L]
        acc_free = [sem(f"acc_free{l}") for l in L]
        ln_v = [sem(f"ln_v{l}") for l in L]
        ln_s = [sem(f"ln_s{l}") for l in L]
        hid_ready = [sem(f"hid_ready{l}") for l in L]
        ht_pe = [sem(f"ht_pe{l}") for l in L]
        ht_ready = [sem(f"ht_ready{l}") for l in L]
        wh_ready = [sem(f"wh_ready{l}") for l in L]
        wh_copied = [sem(f"wh_copied{l}") for l in L]
        s1_copied = [sem(f"s1_copied{l}") for l in L]
        mx_v = [sem(f"mx_v{l}") for l in L]
        mx_pe = [sem(f"mx_pe{l}") for l in L]
        exps = [sem(f"exps{l}") for l in L]
        q_ready = [sem(f"q_ready{l}") for l in L]
        g_ready = [sem(f"g_ready{l}") for l in L]
        rows_in = [sem(f"rows_in{i}") for i in range(2)]
        fin_v = [sem(f"fin_v{l}") for l in L]
        fin_s = [sem(f"fin_s{l}") for l in L]
        x_new = [sem(f"x_new{l}") for l in L]
        out_done = sem("out_done")
        col_zeroed = sem("col_zeroed")
        w_ready = sem("w_ready")
        link_sem = sem("link_sem")

        ADJ_SLOTS, ROW_SLOT_STEPS, PT_SLOTS, COL_SLOTS = 4, CT, 2, BODY

        x_v = x.rearrange("(b t p) f -> b p t f", p=P, t=BT)
        out_v = out.rearrange("(b t p) f -> b p t f", p=P, t=BT)
        adj_v = adj.rearrange("(b h r p) (c j) -> b h p r c j", p=P, r=HR, h=2, c=NCC * 2)

        block = ctx.enter_context(nc.Block())

        @block.sync
        def _(sp):
            for b in range(NB):
                sp.dma_start(x_sb[:, b * BT:(b + 1) * BT, :], x_v[b]).then_inc(x_in[b], 16)
                if b == 0:
                    for l, (w, a) in enumerate(((w0, a0), (w1, a1))):
                        sp.dma_start(wa[:, l, 0:F], w).then_inc(w_in, 16)
                        with nc.allow_non_contiguous_dma(reason="256 scores weights, once"):
                            sp.dma_start(a_sb[:, l, :], a.rearrange("(k f) o -> f (k o)", k=2)).then_inc(w_in, 16)
            with sp.Fori(0, NB) as ib:
                with sp.Fori(0, NCC) as cc:
                    body = ib * NCC + cc
                    for slot in range(ADJ_SLOTS):
                        ch, half = slot // 2, slot % 2
                        sp.wait_ge(converted, body * 4 + slot + 1)
                        src = adj_v[bass.ds(ib, 1), half, :, :, bass.ds(cc * 2 + ch, 1), :]
                        sp.dma_start(adj_sb[:, slot, :, :], src.rearrange("a p r c j -> p (a r) (c j)")).then_inc(adj_in[slot], 16)
            for slot in range(2):
                sp.wait_ge(converted, NB * NCC * 4 + slot + 1)
                sp.dma_start(adj_sb[:, slot, :, :], adj_v[0, slot, :, :, 0, :]).then_inc(adj_in[slot], 16)
            for ch in range(2):
                sp.wait_ge(stored[ch], 16 * (NB * NCC + 1))
            sp.wait_ge(p_ready[0], NB * NT + COL_SLOTS)
            sp.wait_ge(evacuated, NB * NT + LEAD + PT_SLOTS)
            with sp.Fori(0, NB) as ib:
                with sp.Fori(0, NCC) as cc:
                    body = ib * NCC + cc
                    for ch in range(2):
                        sp.wait_ge(p_ready[1], body * BODY + ch * CT + CT)
                        src = mask_dram[bass.ds(ib, 1), bass.ds(cc * 2 + ch, 1), :, :]
                        sp.dma_start(col_sb[:, ch, :, :], src.rearrange("a c p (t i) -> p (a c t) i", t=CT)).then_inc(mask_in[ch], 16)

        @block.gpsimd
        def _(pool):
            nc.gpsimd.memset(ident[:, :], 0.0).then_inc(const_ready, 1)
            nc.gpsimd.memset(ones[:, :], 1.0).then_inc(const_ready, 1)
            nc.gpsimd.memset(zeros16[:, :], 0.0).then_inc(const_ready, 1)
            pool.wait_ge(const_ready, 3)
            nc.gpsimd.affine_select(out=ident[:, :], in_=ident[:, :], compare_op=ALU.not_equal, fill=1.0, base=0,
                                    pattern=[[-1, P]], channel_multiplier=1).then_inc(const_ready, 1)
            pool.wait_ge(const_ready, 4)
            nc.gpsimd.tensor_copy(ident16[:, :], ident[:, :]).then_inc(const_ready, 1)
            for l in L:
                pool.sem_inc(acc_free[l], 1)
            for l in L:
                with pool.Fori(0, NB) as ib:
                    pool.wait_ge(acc_saved[l], ib + 2)
                    dst = acc_dram[l, bass.ds(ib, 1), :, :].rearrange("a p w -> p (a w)")
                    pool.dma_start(dst, acc_sb[:, :, :].rearrange("p t w -> p (t w)")).then_inc(acc_out[l], 16)
                    pool.wait_ge(acc_out[l], ib * 16 + 16)
                    pool.sem_inc(acc_free[l], 1)
                for b in range(NB):
                    if b:
                        pool.wait_ge(fin_v[l], (2, 1)[l] * b)
                    pool.dma_start(acc_sb[:, :, :].rearrange("p t w -> p (t w)"), acc_dram[l, b]).then_inc(rows_in[l], 16)

        @block.scalar
        def _(act):
            act.sem_inc(evacuated, PT_SLOTS)

            def layernorm_and_project(l):
                for b in range(NB + 1):
                    if b < NB:
                        act.wait_ge(ln_v[l], 5 * b + 2)
                        nc.scalar.activation(sq[:, :, :], hid[:, b % 2], ACT.Square).then_inc(ln_s[l], 1)
                        act.wait_ge(ln_v[l], 5 * b + 4)
                        nc.scalar.activation(st[:, b % 2, 2, :], st[:, b % 2, 1, :], ACT.Sqrt).then_inc(ln_s[l], 1)
                    if b:
                        a = b - 1
                        act.wait_ge(ht_pe[l], a + 1)
                        if a >= 2:
                            act.wait_ge(wh_ready[l], a - 1)
                        for k in range(2):
                            ins = nc.scalar.activation(hT[:, a % 2, k * 512:k * 512 + 512], ps_all[k], ACT.Copy,
                                                       accum_out=hsum[:, k, a:a + 1])
                            ins.then_inc(ht_ready[l], 1)
                        act.wait_ge(wh_ready[l], a + 1)
                        for k in range(2):
                            nc.scalar.activation(q_sb[:, a * BI + k * 512:a * BI + k * 512 + 512], ps_all[5 + k],
                                                 ACT.Copy).then_inc(s1_copied[l], 1)

            def exponentials(l):
                s2 = g_sb[:, :, F:GW].rearrange("p t o -> p (t o)")
                act.wait_ge(mx_v[l], 4)
                nc.scalar.activation(t_sb[:, :], s2, ACT.Exp, bias=mx[:, 2:3], scale=1 - SLOPE).then_inc(exps[l], 1)
                nc.scalar.activation(f_sb[:, :], s2, ACT.Exp, bias=mx[:, 3:4], scale=SLOPE).then_inc(exps[l], 1)
                act.wait_ge(s1_copied[l], 2 * NB)
                for b in range(NB):
                    q = q_sb[:, b * BI:(b + 1) * BI]
                    nc.scalar.activation(q, q, ACT.Exp, bias=mx[:, 2:3], scale=-(1 - SLOPE)).then_inc(exps[l], 1)

            for l in L:
                act.wait_ge(wprep_pe, 3 * l + 1)
                nc.scalar.activation(w_T[:, l, :], ps_all[0][:, 0:P], ACT.Copy).then_inc(wprep_sb, 1)
                act.wait_ge(wprep_pe, 3 * l + 2)
                nc.scalar.activation(w_rep[:, l, :], ps_all[1][:, 0:P], ACT.Copy).then_inc(wprep_sb, 1)
                act.wait_ge(wprep_pe, 3 * l + 3)
                nc.scalar.activation(wa[:, l, F:GW], ps_all[2][:, 0:1], ACT.Copy).then_inc(wprep_sb, 1)

            layernorm_and_project(0)
            exponentials(0)

            act.wait_ge(col_zeroed, 1)
            for ch in range(2):
                act.dma_start(mask_dram[NB - 1, 2 * NCC - 2 + ch], col_sb[:, ch, :, :].rearrange("p t i -> p (t i)")).then_inc(stored[ch], 16)

            def evacuate(k, step):
                act.wait_ge(transposed, step + 1 + ROW_SLOT_STEPS)
                act.wait_ge(p_ready[0], step + 1)
                nc.scalar.activation(col_sb[:, k // CT, k % CT, :], pt[k % 2], ACT.Copy).then_inc(evacuated, 1)

            def store(ch, ib, cc, steps_done):
                act.wait_ge(evacuated, steps_done + PT_SLOTS)
                dst = mask_dram[bass.ds(ib, 1), bass.ds(cc * 2 + ch, 1), :, :].rearrange("a c p w -> p (a c w)")
                act.dma_start(dst, col_sb[:, ch, :, :].rearrange("p t i -> p (t i)")).then_inc(stored[ch], 16)

            with act.Fori(0, NB) as ib:
                with act.Fori(0, NCC) as cc:
                    body = ib * NCC + cc
                    for k in range(BODY):
                        if k % CT == 0:
                            act.wait_ge(stored[k // CT], body * 16 + 16)
                        evacuate(k, body * BODY + k)
                        if k == CT:
                            store(0, ib, cc, body * BODY + CT)
                    store(1, ib, cc, body * BODY + BODY)
            act.wait_ge(stored[0], 16 * (NB * NCC + 1))
            for k in range(LEAD):
                evacuate(k, NB * NCC * BODY + k)

            for b in range(NB):
                act.wait_ge(fin_v[0], 2 * b + 2)
                nc.scalar.activation(ex[:, :, :], corr[:, :, :], ACT.Exp).then_inc(fin_s[0], 1)
            layernorm_and_project(1)
            exponentials(1)
            for b in range(NB):
                act.wait_ge(x_new[1], b + 1)
                act.dma_start(out_v[b], x_sb[:, b * BT:(b + 1) * BT, :]).then_inc(out_done, 16)
            act.wait_ge(out_done, 16 * NB)

        @block.vector
        def _(dve):
            nc.vector.memset(col_sb[:, :, :, :], 0).then_inc(col_zeroed, 1)
            dve.sem_inc(converted, ADJ_SLOTS)
            for l in L:
                dve.sem_inc(p_ready[l], COL_SLOTS)
                dve.sem_inc(acc_saved[l], 1)

            chain = [0]

            def link(ins):
                chain[0] += 1
                ins.then_inc(link_sem, 1)
                dve.wait_ge(link_sem, chain[0])

            def layernorm_and_project(l):
                for b in range(NB + 1):
                    if b < NB:
                        s = b % 2
                        xb = x_sb[:, b * BT:(b + 1) * BT, :]
                        if l == 0:
                            dve.wait_ge(x_in[b], 16)
                        else:
                            dve.wait_ge(x_new[0], b + 1)
                        nc.vector.tensor_reduce(st[:, s, 0, :], xb, AX_X, ALU.add).then_inc(ln_v[l], 1)
                        dve.wait_ge(ln_v[l], 5 * b + 1)
                        if b >= 2:
                            dve.wait_ge(ht_pe[l], b - 1)
                        nc.vector.scalar_tensor_tensor(out=hid[:, s], in0=st[:, s, 0, :].to_broadcast([P, BT, F]), scalar=-1.0 / F,
                                                       in1=xb, op0=ALU.mult, op1=ALU.add).then_inc(ln_v[l], 1)
                        dve.wait_ge(ln_s[l], 2 * b + 1)
                        nc.vector.tensor_reduce(st[:, s, 3, :], sq[:, :, :], AX_X, ALU.add).then_inc(ln_v[l], 1)
                        dve.wait_ge(ln_v[l], 5 * b + 3)
                        nc.vector.tensor_scalar(st[:, s, 1, :], st[:, s, 3, :], 1.0 / F, EPS, ALU.mult, ALU.add).then_inc(ln_v[l], 1)
                        dve.wait_ge(ln_s[l], 2 * b + 2)
                        nc.vector.reciprocal(st[:, s, 3, :], st[:, s, 2, :]).then_inc(ln_v[l], 1)
                        dve.wait_ge(ln_v[l], 5 * b + 5)
                        nc.vector.scalar_tensor_tensor(out=hid[:, s], in0=hid[:, s], scalar=0.0,
                                                       in1=st[:, s, 3, :].to_broadcast([P, BT, F]),
                                                       op0=ALU.max, op1=ALU.mult).then_inc(hid_ready[l], 1)
                    if b:
                        a = b - 1
                        dve.wait_ge(wh_ready[l], a + 1)
                        for k in range(BANKS):
                            n = min(PER_BANK, BT - k * PER_BANK)
                            t0 = a * BT + k * PER_BANK
                            nc.vector.tensor_copy(g_sb[:, t0:t0 + n, :], ps_all[2 + k][:, 0:n * GW].rearrange("p (t w) -> p t w", w=GW)
                                                  ).then_inc(wh_copied[l], 1)

            def scale_operands(l):
                s2 = g_sb[:, :, F:GW].rearrange("p t o -> p (t o)")
                dve.wait_ge(wh_copied[l], BANKS * NB)
                nc.vector.tensor_reduce(mx[:, 0:1], s2, AX_X, ALU.max).then_inc(mx_v[l], 1)
                nc.vector.tensor_reduce(st[:, 0, 0, 0:1], hsum[:, :, :].rearrange("p k b -> p (k b)"), AX_X, ALU.add).then_inc(g_ready[l], 1)
                dve.wait_ge(g_ready[l], 1)
                nc.vector.tensor_scalar(hs_rep[:, :], ones[:, :], st[:, 0, 0, 0:1], 1.0 / N, ALU.mult, ALU.mult).then_inc(g_ready[l], 1)
                dve.wait_ge(mx_pe[l], 1)
                nc.vector.tensor_reduce(mx[0:1, 1:2], ps_all[7][0:1, 0:P], AX_X, ALU.max).then_inc(mx_v[l], 1)
                dve.wait_ge(mx_pe[l], 3)
                nc.vector.tensor_scalar(mx[:, 2:3], ps_all[0][:, 0:1], -(1 - SLOPE), None, ALU.mult).then_inc(mx_v[l], 1)
                nc.vector.tensor_scalar(mx[:, 3:4], ps_all[0][:, 0:1], -SLOPE, None, ALU.mult).then_inc(mx_v[l], 1)
                nc.vector.tensor_copy(wh_mean[:, :], ps_all[1][:, 0:F]).then_inc(g_ready[l], 1)
                dve.wait_ge(exps[l], 3)
                nc.vector.tensor_scalar(q_sb[:, 0:BI], q_sb[:, 0:BI], 1.0, None, ALU.min).then_inc(q_ready[l], 1)
                for b in range(NB):
                    fb = f_sb[:, b * BT:(b + 1) * BT]
                    gb = g_sb[:, b * BT:(b + 1) * BT, :]
                    nc.vector.tensor_tensor(gb[:, :, 0:F], gb[:, :, 0:F], fb.to_broadcast([P, BT, F]), ALU.mult).then_inc(g_ready[l], 1)
                nc.vector.tensor_copy(s2, f_sb[:, :]).then_inc(g_ready[l], 1)
                dve.wait_ge(exps[l], 2 + NB)
                nc.vector.tensor_scalar(q_sb[:, BI:N], q_sb[:, BI:N], 1.0, None, ALU.min).then_inc(q_ready[l], 1)

            def convert(slot, value, chunk_free):
                dve.wait_ge(adj_in[slot], value)
                dve.wait_ge(transposed, chunk_free)
                half = slot % 2
                nc.vector.tensor_scalar(row_sb[:, slot // 2, half * HR:(half + 1) * HR, :], adj_sb[:, slot, :, :], 0, None,
                                        ALU.is_gt).then_inc(converted, 1)

            def make_p(l, k, ib, cc, step):
                dve.wait_ge(p_used[l], step + 1)
                tile = cc * BODY + k
                nc.vector.scalar_tensor_tensor(out=p_sb[:, k % PR, :], in0=q_sb[:, bass.ds(ib * BI, BI)],
                                               scalar=t_sb[:, bass.ds(tile, 1)], in1=col_sb[:, k // CT, k % CT, :],
                                               op0=ALU.max, op1=ALU.mult).then_inc(p_ready[l], 1)

            def save_accumulators(l, ib):
                dve.wait_ge(acc_free[l], ib + 1)
                dve.wait_ge(p_used[l], ib * NT + NT + PR)
                nc.vector.tensor_copy(acc_sb[:, :, :].rearrange("p (k t) w -> p k (t w)", k=BANKS),
                                      psum[:, 0:BANKS, 0:PER_BANK * GW]).then_inc(acc_saved[l], 1)

            def finish_block(l, b):
                dve.wait_ge(rows_in[l], 16 * (b + 1))
                D = acc_sb[:, 0:BT, F:GW].rearrange("p t o -> p (t o)")
                link(nc.vector.tensor_scalar(den[:, 0, :], D, 0.0, None, ALU.is_equal))
                link(nc.vector.tensor_tensor(den[:, 1, :], D, den[:, 0, :], ALU.add))
                link(nc.vector.reciprocal(den[:, 2, :], den[:, 1, :]))
                for t in range(BT):
                    ins = nc.vector.scalar_tensor_tensor(out=hp[:, t, :], in0=wh_mean[:, :], scalar=den[:, 0, t:t + 1],
                                                         in1=acc_sb[:, t, 0:F], op0=ALU.mult, op1=ALU.add)
                link(ins)
                nc.vector.tensor_tensor(hp[:, :, :], hp[:, :, :], den[:, 2, :].to_broadcast([P, BT, F]), ALU.mult).then_inc(fin_v[l], 1)
                dve.wait_ge(fin_v[l], (2, 1)[l] * b + 1)
                xb = x_sb[:, b * BT:(b + 1) * BT, :]
                if l == 0:
                    nc.vector.tensor_scalar(corr[:, :, :], hp[:, :, :], 0.0, None, ALU.min).then_inc(fin_v[l], 1)
                    dve.wait_ge(fin_s[0], b + 1)
                    link(nc.vector.scalar_tensor_tensor(out=hp[:, :, :], in0=hp[:, :, :], scalar=0.0, in1=ex[:, :, :],
                                                        op0=ALU.max, op1=ALU.add))
                    nc.vector.scalar_tensor_tensor(out=xb, in0=hp[:, :, :], scalar=-1.0, in1=xb,
                                                   op0=ALU.add, op1=ALU.add).then_inc(x_new[l], 1)
                else:
                    nc.vector.tensor_tensor(xb, xb, hp[:, :, :], ALU.add).then_inc(x_new[l], 1)

            dve.wait_ge(w_in, 64)
            dve.wait_ge(const_ready, 5)
            for l in L:
                nc.vector.tensor_scalar(a_rep[:, l, :], ones[:, :], a_sb[:, l, 0:1], None, ALU.mult).then_inc(w_ready, 1)

            layernorm_and_project(0)
            scale_operands(0)
            dve.wait_ge(q_ready[0], 2)
            convert_first = [(0, 16), (1, 16)]
            for slot, value in convert_first:
                dve.wait_ge(adj_in[slot], value)
                nc.vector.tensor_scalar(row_sb[:, 0, slot * HR:(slot + 1) * HR, :], adj_sb[:, slot, :, :], 0, None,
                                        ALU.is_gt).then_inc(converted, 1)
            with dve.Fori(0, NB) as ib:
                with dve.Fori(0, NCC) as cc:
                    body = ib * NCC + cc
                    for k in range(BODY):
                        dve.wait_ge(evacuated, body * BODY + k + 1 + PT_SLOTS)
                        make_p(0, k, ib, cc, body * BODY + k)
                        if k < 2:
                            convert(2 + k, body * 16 + 16, body * BODY + ROW_SLOT_STEPS)
                        if k in (CT, CT + 1):
                            convert(k - CT, body * 16 + 32, body * BODY + CT + ROW_SLOT_STEPS)
                save_accumulators(0, ib)
            for b in range(NB):
                finish_block(0, b)
            layernorm_and_project(1)
            scale_operands(1)
            dve.wait_ge(q_ready[1], 2)
            with dve.Fori(0, NB) as ib:
                with dve.Fori(0, NCC) as cc:
                    body = ib * NCC + cc
                    for k in range(BODY):
                        if k % CT == 0:
                            dve.wait_ge(mask_in[k // CT], body * 16 + 16)
                        make_p(1, k, ib, cc, body * BODY + k)
                save_accumulators(1, ib)
            for b in range(NB):
                finish_block(1, b)

        @block.tensor
        def _(pe):
            pe.sem_inc(transposed, ROW_SLOT_STEPS)
            for l in L:
                pe.sem_inc(p_used[l], PR)
            pe.wait_ge(w_in, 64)
            pe.wait_ge(const_ready, 5)
            for l in L:
                if l:
                    pe.wait_ge(wprep_sb, 3 * l)
                pe.transpose(ps_all[0][:, 0:P], wa[:, l, 0:F], ident[:, :]).then_inc(wprep_pe, 1)
                pe.wait_ge(wprep_sb, 3 * l + 1)
                pe.wait_ge(w_ready, l + 1)
                pe.matmul(ps_all[1][:, 0:P], w_T[:, l, :], a_rep[:, l, :], start=True, stop=True).then_inc(wprep_pe, 1)
                pe.matmul(ps_all[2][:, 0:1], w_T[:, l, :], a_sb[:, l, 1:2], start=True, stop=True).then_inc(wprep_pe, 1)
            pe.wait_ge(wprep_sb, 6)

            def layernorm_and_project(l):
                for b in range(NB):
                    s = b % 2
                    pe.wait_ge(hid_ready[l], b + 1)
                    if b:
                        pe.wait_ge(ht_ready[l], 2 * b)
                    for t in range(BT):
                        mm = pe.transpose(ps_all[t // 4][:, (t % 4) * P:(t % 4 + 1) * P], hid[:, s, t, :], ident[:, :])
                    mm.then_inc(ht_pe[l], 1)
                    pe.wait_ge(ht_ready[l], 2 * b + 2)
                    if b:
                        pe.wait_ge(wh_copied[l], BANKS * b)
                        pe.wait_ge(s1_copied[l], 2 * b)
                    for t in range(BT):
                        c = (t % PER_BANK) * GW
                        pe.matmul(ps_all[2 + t // PER_BANK][:, c:c + GW], hT[:, s, t * P:(t + 1) * P], wa[:, l, :],
                                  start=(t % PER_BANK == 0), stop=True, skip_group_check=True)
                    for k in range(2):
                        mm = pe.matmul(ps_all[5 + k], w_rep[:, l, :], hT[:, s, k * 512:(k + 1) * 512], start=True, stop=True)
                    mm.then_inc(wh_ready[l], 1)

            def share_maximum(l):
                pe.wait_ge(mx_v[l], 1)
                pe.transpose(ps_all[7][0:1, 0:P], mx[:, 0:1], ident[:, :]).then_inc(mx_pe[l], 1)
                pe.wait_ge(mx_v[l], 2)
                pe.matmul(ps_all[0][:, 0:1], ones[0:1, :], mx[0:1, 1:2], start=True, stop=True).then_inc(mx_pe[l], 1)
                pe.wait_ge(g_ready[l], 2)
                pe.matmul(ps_all[1][:, 0:F], hs_rep[:, :], wa[:, l, 0:F], start=True, stop=True).then_inc(mx_pe[l], 1)

            def transposes(k, ready):
                if k % CT == 0:
                    pe.wait_ge(converted, ready[0])
                pe.wait_ge(evacuated, ready[1])
                for r in range(BT):
                    mm = pe.transpose(pt[k % 2][:, r * P:(r + 1) * P],
                                      row_sb[:, k // CT, r, (k % CT) * P:(k % CT + 1) * P], ident16[:, :])
                mm.then_inc(transposed, 1)

            def open_accumulators(l, ib):
                pe.wait_ge(acc_saved[l], ib + 1)
                for k in range(BANKS):
                    pe.matmul(ps_all[k][:, 0:PER_BANK * GW], zeros16[:, 0:P], zeros16[:, :], start=True, stop=False,
                              skip_group_check=True)

            def products(l, k, cc, step):
                pe.wait_ge(p_ready[l], step + 1 + COL_SLOTS)
                g = g_sb[:, bass.ds(cc * BODY + k, 1), :].rearrange("p t w -> p (t w)")
                for r in range(BT):
                    mm = pe.matmul(acc_tile(r), p_sb[:, k % PR, r * P:(r + 1) * P], g, start=False, stop=False,
                                   skip_group_check=True)
                mm.then_inc(p_used[l], 1)
                return mm

            layernorm_and_project(0)
            share_maximum(0)
            pe.wait_ge(g_ready[0], 4 + NB)
            for k in range(LEAD):
                transposes(k, (2 + ADJ_SLOTS, k + 1))
            with pe.Fori(0, NB) as ib:
                open_accumulators(0, ib)
                with pe.Fori(0, NCC) as cc:
                    body = ib * NCC + cc
                    for k in range(BODY):
                        ahead = (k + LEAD) % BODY
                        chunk = 2 * body + (k + LEAD) // CT
                        transposes(ahead, (2 * chunk + 2 + ADJ_SLOTS, body * BODY + k + LEAD + 1))
                        products(0, k, cc, body * BODY + k)
            layernorm_and_project(1)
            share_maximum(1)
            pe.wait_ge(g_ready[1], 4 + NB)
            with pe.Fori(0, NB) as ib:
                open_accumulators(1, ib)
                with pe.Fori(0, NCC) as cc:
                    body = ib * NCC + cc
                    for k in range(BODY):
                        products(1, k, cc, body * BODY + k)


_INS = ['x', 'adj', 'L0_gnn_W', 'L0_gnn_a', 'L1_gnn_W', 'L1_gnn_a']
_OUTS = [((8192, 128), 'float32')]


def kernel(**inputs):
    import numpy as _np
    import concourse.bacc as _bacc
    from concourse import mybir as _mybir
    from concourse.bass_utils import run_bass_kernel_spmd as _run

    nc = _bacc.Bacc("TRN2", target_bir_lowering=False, num_devices=1)
    arrays, args = {}, []
    for name in _INS:
        a = _np.ascontiguousarray(inputs[name])
        arrays[f"in_{name}_dram"] = a
        args.append(nc.dram_tensor(f"in_{name}_dram", a.shape, _mybir.dt.from_np(a.dtype), kind="ExternalInput").ap())
    for i, (shape, dtype) in enumerate(_OUTS):
        dt = _mybir.dt.from_np(_np.dtype(dtype))
        args.append(nc.dram_tensor(f"out_{i}_dram", shape, dt, kind="ExternalOutput").ap())
    gat_two_layers(nc, *args)
    r = _run(nc, [arrays], core_ids=[0])
    got = tuple(r.results[0][f"out_{i}_dram"] for i in range(len(_OUTS)))
    return got[0]
```

```python
from contextlib import ExitStack

import concourse.bass as bass
from concourse import mybir

ALU = mybir.AluOpType
ACT = mybir.ActivationFunctionType
AX_X = mybir.AxisListType.X
F32 = mybir.dt.float32
BF16 = mybir.dt.bfloat16
U8 = mybir.dt.uint8
I32 = mybir.dt.int32

P = 128
SLOPE = 0.2
EPS = 1e-5


def gat_two_layers(nc, x, adj, w0, a0, w1, a1, out):
    N, F = x.shape
    NT = N // P
    BT = 8
    BI = BT * P
    NB = NT // BT
    CT = 4
    CJ = CT * P
    BODY = 2 * CT
    NCC = NT // BODY
    EARLY = 3
    GW = F + 1
    PW = F + 2
    PER_BANK = 3
    BANKS = 3
    SLOTS = BANKS * PER_BANK
    LEAD = 3
    PR = 4
    HR = BT // 2
    UNITS = NT // HR
    TINY = 2.0 ** -100

    ctx = ExitStack()
    with ctx:
        def sb(name, shape, dt=F32):
            return ctx.enter_context(nc.sbuf_tensor(name, shape, dt))

        def sem(name):
            return ctx.enter_context(nc.semaphore(name))

        g_sb = [sb(f"g{l}_sb", [P, NT, PW]) for l in range(2)]
        q_sb = sb("q_sb", [P, N])
        x_all = q_sb[:, :].rearrange("p (t f) -> p t f", f=F)
        adj_sb = sb("adj_sb", [P, 4, HR, CJ], I32)
        row_sb = sb("row_sb", [P, 2, BT, CJ], BF16)
        col_sb = sb("col_sb", [P, 2, CT, BI], U8)
        p_sb = sb("p_sb", [P, PR, BI])
        hp = sb("hp", [P, SLOTS, F])
        xb = sb("xb", [P, BT, F])
        xn = sb("xn", [P, BT, F])
        ex = sb("ex", [P, BT, F])
        rl = sb("rl", [P, BT, F])
        hid = sb("hid", [P, 2, HR, F])
        hT = sb("hT", [P, 2, HR * P])
        rec = sb("rec", [P, SLOTS])
        bn = sb("bn", [P, 2 * BT, 6])
        mv = sb("mv", [P, 2 * BT, 2])
        ve = sb("ve", [P, 2 * BT])
        rstd = sb("rstd", [P, 2 * BT])
        eps_t = sb("eps_t", [P, BT])
        mhalf = sb("mhalf", [P, BT])
        t_sb = sb("t_sb", [P, NT])
        f_sb = sb("f_sb", [P, NT])
        qc_sb = sb("qc_sb", [P, NT])
        qT_sb = sb("qT_sb", [NT, P])
        wa = sb("wa", [P, 2, PW])
        w_T = sb("w_T", [P, P])
        a_sb = sb("a_sb", [P, 2, 2])
        ident = sb("ident", [P, P])
        ident16 = sb("ident16", [P, P], BF16)
        ones = sb("ones", [P, P])
        tiny16 = sb("tiny16", [P, P], BF16)
        hsum = sb("hsum", [P, UNITS])
        hs = sb("hs", [P, 1])
        hs_rep = sb("hs_rep", [P, P])
        mean_v = sb("mean_v", [P, GW])
        m_hi = sb("m_hi", [P, GW], BF16)
        m_mid = sb("m_mid", [P, GW], BF16)
        rest1 = sb("rest1", [P, GW])
        rest2 = sb("rest2", [P, GW])
        mean16 = sb("mean16", [P, PER_BANK, GW], BF16)
        mx = sb("mx", [P, 4])

        psum = ctx.enter_context(nc.psum_tensor("psum", [P, 8, 512], F32))
        bank = [psum[:, i, :] for i in range(8)]
        pt = [bank[3].bitcast(BF16), bank[4].bitcast(BF16)]
        PROJECTION_BANKS = [(5, 6, 7), (2, 3, 4)]
        SETS = [2, 1]

        mask_dram = nc.dram_tensor("mask_cols", [NB, NCC * 2, P, CT * BI], U8, kind="Internal").ap()
        x1_dram = nc.dram_tensor("x1_rows", [NB, P, BT, F], F32, kind="Internal").ap()
        q_dram = [nc.dram_tensor(f"q_row{l}", [NT, P], F32, kind="Internal").ap() for l in range(2)]

        def acc_tile(r):
            return bank[r // PER_BANK][:, (r % PER_BANK) * GW:(r % PER_BANK) * GW + GW]

        L = range(2)
        x_first, x_rest, w_in = sem("x_first"), sem("x_rest"), sem("w_in")
        const_ready, half_ready, col_zeroed = sem("const_ready"), sem("half_ready"), sem("col_zeroed")
        wprep_pe, wprep_sb = sem("wprep_pe"), sem("wprep_sb")
        adj_in = [sem(f"adj_in{i}") for i in range(4)]
        converted = sem("converted")
        transposed = sem("transposed")
        evacuated = sem("evacuated")
        stored = [sem(f"stored{i}") for i in range(2)]
        mask_in = [sem(f"mask_in{i}") for i in range(2)]
        p_ready = [sem(f"p_ready{l}") for l in L]
        p_used = [sem(f"p_used{l}") for l in L]
        rec_done = [sem(f"rec_done{l}") for l in L]
        acc_saved = [sem(f"acc_saved{l}") for l in L]
        xb_in = [sem(f"xb_in{l}") for l in L]
        elu_s, elu_v, xn_ready = sem("elu_s"), sem("elu_v"), [sem(f"xn_ready{l}") for l in L]
        xn_out = [sem(f"xn_out{l}") for l in L]
        xn_free = [sem(f"xn_free{l}") for l in L]
        stats_v = [sem(f"stats_v{l}") for l in L]
        parts_seen = sem("parts_seen")
        stats_done = [sem(f"stats_done{l}") for l in L]
        eps_added = [sem(f"eps_added{l}") for l in L]
        rstd_ready = [sem(f"rstd_ready{l}") for l in L]
        hid_ready = [sem(f"hid_ready{l}") for l in L]
        ht_pe = [sem(f"ht_pe{l}") for l in L]
        ht_ready = [sem(f"ht_ready{l}") for l in L]
        wh_ready = [sem(f"wh_ready{l}") for l in L]
        wh_copied = [sem(f"wh_copied{l}") for l in L]
        mx_v, mx_pe = [sem(f"mx_v{l}") for l in L], [sem(f"mx_pe{l}") for l in L]
        hs_v = [sem(f"hs_v{l}") for l in L]
        exps = [sem(f"exps{l}") for l in L]
        q_v = [sem(f"q_v{l}") for l in L]
        q_pe = [sem(f"q_pe{l}") for l in L]
        q_out, q_first, q_rest = ([sem(f"{n}{l}") for l in L] for n in ("q_out", "q_first", "q_rest"))
        f_placed = [sem(f"f_placed{l}") for l in L]
        g_ready = [sem(f"g_ready{l}") for l in L]
        mean_s = [sem(f"mean_s{l}") for l in L]

        ADJ_SLOTS, ROW_SLOT_STEPS, PT_SLOTS, COL_SLOTS, HID_SLOTS = 4, CT, 2, BODY, 2

        x_v = x.rearrange("(b t p) f -> b p t f", p=P, t=BT)
        xt_v = x.rearrange("(t p) f -> p t f", p=P)
        out_v = out.rearrange("(b t p) f -> b p t f", p=P, t=BT)
        adj_v = adj.rearrange("(b h r p) (c j) -> b h p r c j", p=P, r=HR, h=2, c=NCC * 2)

        block = ctx.enter_context(nc.Block())

        @block.sync
        def _(sp):
            FIRST = 2 * BT
            sp.dma_start(x_all[:, 0:FIRST, :], xt_v[:, 0:FIRST, :]).then_inc(x_first, 16)
            for l, (w, a) in enumerate(((w0, a0), (w1, a1))):
                sp.dma_start(wa[:, l, 0:F], w).then_inc(w_in, 16)
                with nc.allow_non_contiguous_dma(reason="256 score weights, once"):
                    sp.dma_start(a_sb[:, l, :], a.rearrange("(k f) o -> f (k o)", k=2)).then_inc(w_in, 16)
            sp.dma_start(x_all[:, FIRST:NT, :], xt_v[:, FIRST:NT, :]).then_inc(x_rest, 16)
            with sp.Fori(0, NB) as ib:
                with sp.Fori(0, NCC) as cc:
                    body = ib * NCC + cc
                    for slot in range(ADJ_SLOTS):
                        ch, half = slot // 2, slot % 2
                        sp.wait_ge(converted, body * 4 + slot + 1)
                        src = adj_v[bass.ds(ib, 1), half, :, :, bass.ds(cc * 2 + ch, 1), :]
                        sp.dma_start(adj_sb[:, slot, :, :], src.rearrange("a p r c j -> p (a r) (c j)")).then_inc(adj_in[slot], 16)
            for slot in range(2):
                sp.wait_ge(converted, NB * NCC * 4 + slot + 1)
                sp.dma_start(adj_sb[:, slot, :, :], adj_v[0, slot, :, :, 0, :]).then_inc(adj_in[slot], 16)
            for ch in range(2):
                sp.wait_ge(stored[ch], 16 * (NB * NCC + 1))
            sp.wait_ge(p_ready[0], NB * NT + COL_SLOTS)
            sp.wait_ge(evacuated, NB * NT + LEAD + PT_SLOTS)
            with sp.Fori(0, NB) as ib:
                with sp.Fori(0, NCC) as cc:
                    body = ib * NCC + cc
                    for ch in range(2):
                        sp.wait_ge(p_ready[1], body * BODY + ch * CT + CT)
                        src = mask_dram[bass.ds(ib, 1), bass.ds(cc * 2 + ch, 1), :, :]
                        sp.dma_start(col_sb[:, ch, :, :], src.rearrange("a c p (t i) -> p (a c t) i", t=CT)).then_inc(mask_in[ch], 16)

        @block.gpsimd
        def _(pool):
            nc.gpsimd.memset(eps_t[:, :], EPS).then_inc(half_ready, 1)
            nc.gpsimd.memset(mhalf[:, :], -0.5).then_inc(half_ready, 1)
            nc.gpsimd.memset(ident[:, :], 0.0).then_inc(const_ready, 1)
            nc.gpsimd.memset(ones[:, :], 1.0).then_inc(const_ready, 1)
            nc.gpsimd.memset(tiny16[:, :], TINY).then_inc(const_ready, 1)
            pool.wait_ge(half_ready, 2)
            pool.wait_ge(const_ready, 3)
            nc.gpsimd.affine_select(out=ident[:, :], in_=ident[:, :], compare_op=ALU.not_equal, fill=1.0, base=0,
                                    pattern=[[-1, P]], channel_multiplier=1).then_inc(const_ready, 1)
            pool.wait_ge(const_ready, 4)
            nc.gpsimd.tensor_copy(ident16[:, :], ident[:, :]).then_inc(const_ready, 1)
            pool.sem_inc(xn_free[0], 1)

            def inverse_deviation(l, side, count):
                s = slice(side * BT, side * BT + BT)
                pool.wait_ge(stats_done[l], count)
                nc.gpsimd.tensor_tensor(ve[:, s], mv[:, s, 1:2].rearrange("p t o -> p (t o)"), eps_t[:, :], ALU.add).then_inc(eps_added[l], 1)
                pool.wait_ge(eps_added[l], count)
                nc.gpsimd.tensor_tensor(rstd[:, s], ve[:, s], mhalf[:, :], ALU.pow).then_inc(rstd_ready[l], 1)

            def spread_q(l):
                pool.wait_ge(q_v[l], 2)
                pool.dma_start(q_dram[l], qT_sb[:, :]).then_inc(q_out[l], 16)
                pool.wait_ge(q_out[l], 16)
                row = q_dram[l].rearrange("t p -> (t p)")
                pool.dma_start(q_sb[:, 0:BI], row[0:BI].partition_broadcast(P)).then_inc(q_first[l], 16)
                if NB > 1:
                    pool.dma_start(q_sb[:, BI:N], row[BI:N].partition_broadcast(P)).then_inc(q_rest[l], 16)

            with pool.Fori(0, NB // 2) as pair:
                for side in range(2):
                    inverse_deviation(0, side, pair * 2 + side + 1)
            spread_q(0)
            with pool.Fori(0, NB) as e:
                pool.dma_start(xb[:, :, :], x_v[bass.ds(e, 1)].rearrange("a p t f -> p (a t) f")).then_inc(xb_in[0], 16)
                inverse_deviation(1, 0, e + 1)
                pool.dma_start(x1_dram[bass.ds(e, 1)].rearrange("a p t f -> p (a t) f"), xn[:, :, :]).then_inc(xn_out[0], 16)
                pool.wait_ge(xn_out[0], e * 16 + 16)
                pool.sem_inc(xn_free[0], 1)
            spread_q(1)

        @block.scalar
        def _(act):
            act.sem_inc(evacuated, PT_SLOTS)
            for l in L:
                act.sem_inc(ht_ready[l], SETS[l])
                act.sem_inc(wh_copied[l], SETS[l])
            for l in L:
                act.wait_ge(wprep_pe, 2 * l + 1)
                nc.scalar.activation(w_T[:, :], bank[0][:, 0:P], ACT.Copy).then_inc(wprep_sb, 1)
                act.wait_ge(wprep_pe, 2 * l + 2)
                nc.scalar.activation(wa[:, l, F:PW], bank[1][:, 0:2], ACT.Copy).then_inc(wprep_sb, 1)

            def relu_half(l, unit, half, banks):
                act.wait_ge(ht_pe[l], unit + 1 + HID_SLOTS)
                act.wait_ge(wh_ready[l], unit + 1)
                nc.scalar.activation(hT[:, half, :], bank[banks[0]], ACT.Relu,
                                     accum_out=hsum[:, bass.ds(unit, 1)]).then_inc(ht_ready[l], 1)

            def copy_projection(l, unit, banks):
                act.wait_ge(wh_ready[l], unit + 1 + 2)
                g = g_sb[l]
                nc.scalar.activation(g[:, bass.ds(unit * HR, 3), :], bank[banks[1]][:, 0:3 * PW].rearrange("p (t w) -> p t w", w=PW), ACT.Copy)
                nc.scalar.activation(g[:, bass.ds(unit * HR + 3, 1), :], bank[banks[2]][:, 0:PW].rearrange("p (t w) -> p t w", w=PW),
                                     ACT.Copy).then_inc(wh_copied[l], 1)

            def exponentials(l):
                s1 = g_sb[l][:, :, F:F + 1].rearrange("p t o -> p (t o)")
                s2 = g_sb[l][:, :, F + 1:PW].rearrange("p t o -> p (t o)")
                act.wait_ge(mx_v[l], 4)
                nc.scalar.activation(qc_sb[:, :], s1, ACT.Exp, bias=mx[:, 2:3], scale=-(1 - SLOPE)).then_inc(exps[l], 1)
                nc.scalar.activation(f_sb[:, :], s2, ACT.Exp, bias=mx[:, 3:4], scale=SLOPE).then_inc(exps[l], 1)
                nc.scalar.activation(t_sb[:, :], s2, ACT.Exp, bias=mx[:, 2:3], scale=1 - SLOPE).then_inc(exps[l], 1)

            with act.Fori(0, NB // 2) as pair:
                for k in range(4):
                    relu_half(0, pair * 4 + k, k % 2, PROJECTION_BANKS[k % 2])
                    if k:
                        copy_projection(0, pair * 4 + k - 1, PROJECTION_BANKS[(k - 1) % 2])
                copy_projection(0, pair * 4 + 3, PROJECTION_BANKS[1])
            exponentials(0)

            act.wait_ge(col_zeroed, 1)
            for ch in range(2):
                act.dma_start(mask_dram[NB - 1, 2 * NCC - 2 + ch], col_sb[:, ch, :, :].rearrange("p t i -> p (t i)")).then_inc(stored[ch], 16)

            def evacuate(k, step):
                act.wait_ge(transposed, step + 1 + ROW_SLOT_STEPS)
                act.wait_ge(p_ready[0], step + 1)
                nc.scalar.activation(col_sb[:, k // CT, k % CT, :], pt[k % 2], ACT.Copy).then_inc(evacuated, 1)

            def store(ch, ib, cc, steps_done):
                act.wait_ge(evacuated, steps_done + PT_SLOTS)
                dst = mask_dram[bass.ds(ib, 1), bass.ds(cc * 2 + ch, 1), :, :].rearrange("a c p w -> p (a c w)")
                act.dma_start(dst, col_sb[:, ch, :, :].rearrange("p t i -> p (t i)")).then_inc(stored[ch], 16)

            def elu_parts(e, part):
                act.wait_ge(acc_saved[0], e + 1)
                o, fn = ((ex, ACT.Exp), (rl, ACT.Relu))[part]
                nc.scalar.activation(o[:, :, :], hp[:, 0:BT, :], fn).then_inc(elu_s, 1)

            def masks_out(ib, cc, early=None):
                body = ib * NCC + cc
                for k in range(BODY):
                    if k % CT == 0:
                        act.wait_ge(stored[k // CT], body * 16 + 16)
                    evacuate(k, body * BODY + k)
                    if k == CT:
                        store(0, ib, cc, body * BODY + CT)
                    if early is not None:
                        at, e = early * BODY + k, ib - 1
                        if at == 4 or at == 5:
                            elu_parts(e, at - 4)
                        if at == 16 or at == 20:
                            relu_half(1, e * 2 + (at - 16) // 4, (at - 16) // 4, PROJECTION_BANKS[0])
                        if at == 19 or at == 23:
                            copy_projection(1, e * 2 + (at - 19) // 4, PROJECTION_BANKS[0])
                store(1, ib, cc, body * BODY + BODY)

            with act.Fori(0, NCC) as cc:
                masks_out(0, cc)
            with act.Fori(1, NB) as ib:
                for j in range(EARLY):
                    masks_out(ib, j, early=j)
                with act.Fori(EARLY, NCC) as cc:
                    masks_out(ib, cc)
            act.wait_ge(stored[0], 16 * (NB * NCC + 1))
            for k in range(LEAD):
                evacuate(k, NB * NCC * BODY + k)

            e = NB - 1
            for part in range(2):
                elu_parts(e, part)
            for half in range(2):
                relu_half(1, e * 2 + half, half, PROJECTION_BANKS[0])
                copy_projection(1, e * 2 + half, PROJECTION_BANKS[0])
            exponentials(1)

            act.wait_ge(xn_out[0], 16 * NB)
            act.sem_inc(xn_free[1], 1)
            act.dma_start(xb[:, :, :], x1_dram[0]).then_inc(xb_in[1], 16)
            with act.Fori(0, NB - 1) as e:
                act.wait_ge(xn_ready[1], e + 1)
                act.dma_start(out_v[bass.ds(e, 1)].rearrange("a p t f -> p (a t) f"), xn[:, :, :]).then_inc(xn_out[1], 16)
                act.dma_start(xb[:, :, :], x1_dram[bass.ds(e + 1, 1)].rearrange("a p t f -> p (a t) f")).then_inc(xb_in[1], 16)
                act.wait_ge(xn_out[1], e * 16 + 16)
                act.sem_inc(xn_free[1], 1)
            act.wait_ge(xn_ready[1], NB)
            act.dma_start(out_v[NB - 1], xn[:, :, :]).then_inc(xn_out[1], 16)
            act.wait_ge(xn_out[1], 16 * NB)

        @block.vector
        def _(dve):
            nc.vector.memset(col_sb[:, :, :, :].bitcast(F32), 0.0).then_inc(col_zeroed, 1)
            dve.sem_inc(converted, ADJ_SLOTS)
            for l in L:
                dve.sem_inc(p_ready[l], COL_SLOTS)

            def statistics(l, src, side, count):
                for t in range(BT):
                    ins = nc.vector.bn_stats(bn[:, side * BT + t, :], src(t))
                ins.then_inc(stats_v[l], 1)
                dve.wait_ge(stats_v[l], count)
                dve.sem_inc(parts_seen, 1)
                for t in range(BT):
                    ins = nc.vector.bn_aggr(mv[:, side * BT + t, :], bn[:, side * BT + t, :])
                ins.then_inc(stats_done[l], 1)

            def normalise(l, src, side, half, unit):
                dve.wait_ge(ht_pe[l], unit + 1)
                for t in range(HR):
                    i = side * BT + half * HR + t
                    ins = nc.vector.tensor_scalar(hid[:, half, t, :], src(half * HR + t), mv[:, i, 0:1], rstd[:, i:i + 1],
                                                  ALU.subtract, ALU.mult)
                ins.then_inc(hid_ready[l], 1)

            def convert(slot, value, chunk_free=None):
                dve.wait_ge(adj_in[slot], value)
                if chunk_free is not None:
                    dve.wait_ge(transposed, chunk_free)
                half = slot % 2
                nc.vector.tensor_scalar(row_sb[:, slot // 2, half * HR:(half + 1) * HR, :], adj_sb[:, slot, :, :], 0, None,
                                        ALU.is_gt).then_inc(converted, 1)

            def scale_operands(l):
                g = g_sb[l]
                s2 = g[:, :, F + 1:PW].rearrange("p t o -> p (t o)")
                dve.wait_ge(wh_copied[l], UNITS + SETS[l])
                nc.vector.tensor_reduce(mx[:, 0:1], s2, AX_X, ALU.max).then_inc(mx_v[l], 1)
                nc.vector.tensor_reduce(hs[:, :], hsum[:, :], AX_X, ALU.add).then_inc(hs_v[l], 1)
                dve.wait_ge(mx_pe[l], 1)
                nc.vector.tensor_reduce(mx[0:1, 1:2], bank[7][0:1, 0:P], AX_X, ALU.max).then_inc(mx_v[l], 1)
                dve.wait_ge(mx_pe[l], 2)
                nc.vector.tensor_scalar(mx[:, 2:3], bank[6][:, 0:1], -(1 - SLOPE), None, ALU.mult).then_inc(mx_v[l], 1)
                nc.vector.tensor_scalar(mx[:, 3:4], bank[6][:, 0:1], -SLOPE, None, ALU.mult).then_inc(mx_v[l], 1)
                dve.wait_ge(hs_v[l], 1)
                nc.vector.tensor_scalar(hs_rep[:, :], ones[:, :], hs[:, 0:1], 1.0 / N, ALU.mult, ALU.mult).then_inc(hs_v[l], 1)
                dve.wait_ge(exps[l], 1)
                nc.vector.tensor_scalar(qc_sb[:, :], qc_sb[:, :], 1.0, None, ALU.min).then_inc(q_v[l], 1)
                dve.wait_ge(q_pe[l], 1)
                nc.vector.tensor_copy(qT_sb[:, :], bank[7][0:NT, P:2 * P]).then_inc(q_v[l], 1)
                if l == 0:
                    convert(0, 16)
                    convert(1, 16)
                dve.wait_ge(mx_pe[l], 3)
                nc.vector.tensor_copy(mean_v[:, 0:F], bank[5][:, 0:F]).then_inc(mean_s[l], 1)
                nc.vector.memset(mean_v[:, F:GW], 1.0).then_inc(mean_s[l], 1)
                dve.wait_ge(mean_s[l], 2)
                nc.vector.tensor_copy(m_hi[:, :], mean_v[:, :]).then_inc(mean_s[l], 1)
                dve.wait_ge(mean_s[l], 3)
                nc.vector.tensor_tensor(rest1[:, :], mean_v[:, :], m_hi[:, :], ALU.subtract).then_inc(mean_s[l], 1)
                dve.wait_ge(mean_s[l], 4)
                nc.vector.tensor_copy(m_mid[:, :], rest1[:, :]).then_inc(mean_s[l], 1)
                dve.wait_ge(mean_s[l], 5)
                nc.vector.tensor_tensor(rest2[:, :], rest1[:, :], m_mid[:, :], ALU.subtract).then_inc(mean_s[l], 1)
                dve.wait_ge(mean_s[l], 6)
                nc.vector.tensor_scalar(rest2[:, :], rest2[:, :], ident[:, 2:3], None, ALU.mult).then_inc(mean_s[l], 1)
                dve.wait_ge(mean_s[l], 7)
                nc.vector.scalar_tensor_tensor(out=rest1[:, :], in0=m_mid[:, :], scalar=ident[:, 1:2], in1=rest2[:, :],
                                               op0=ALU.mult, op1=ALU.add).then_inc(mean_s[l], 1)
                dve.wait_ge(mean_s[l], 8)
                for k in range(PER_BANK):
                    ins = nc.vector.scalar_tensor_tensor(out=mean16[:, k, :], in0=m_hi[:, :], scalar=ident[:, 0:1], in1=rest1[:, :],
                                                         op0=ALU.mult, op1=ALU.add)
                ins.then_inc(mean_s[l], 1)
                dve.wait_ge(exps[l], 3)
                nc.vector.tensor_copy(g[:, :, F:GW].rearrange("p t o -> p (t o)"), f_sb[:, :]).then_inc(f_placed[l], 1)
                scale_g(l, 0)

            def scale_g(l, part):
                tiles = bass.ds(part * BODY, BODY)
                g = g_sb[l][:, tiles, 0:F]
                nc.vector.tensor_tensor(g, g, f_sb[:, tiles].to_broadcast([P, BODY, F]), ALU.mult).then_inc(g_ready[l], 1)

            def make_p(l, k, ib, cc, step):
                dve.wait_ge(p_used[l], step + 1)
                nc.vector.scalar_tensor_tensor(out=p_sb[:, k % PR, :], in0=q_sb[:, bass.ds(ib * BI, BI)],
                                               scalar=t_sb[:, bass.ds(cc * BODY + k, 1)], in1=col_sb[:, k // CT, k % CT, :],
                                               op0=ALU.max, op1=ALU.mult).then_inc(p_ready[l], 1)

            def save_block(l, e):
                dve.wait_ge(p_used[l], e * NT + NT + PR)
                acc = psum[:, 0:BANKS, 0:PER_BANK * GW].rearrange("p k (t w) -> p k t w", w=GW)
                nc.vector.reciprocal(rec[:, :].rearrange("p (k t) -> p k t", k=BANKS),
                                     acc[:, :, :, F:GW].rearrange("p k t o -> p k (t o)")).then_inc(rec_done[l], 1)
                dve.wait_ge(rec_done[l], e + 1)
                nc.vector.tensor_tensor(hp[:, :, :].rearrange("p (k t) f -> p k t f", k=BANKS), acc[:, :, :, 0:F],
                                        rec[:, :].rearrange("p (k t) -> p k t", k=BANKS).to_broadcast([P, BANKS, PER_BANK, F]),
                                        ALU.mult).then_inc(acc_saved[l], 1)

            def elu_sum(e):
                dve.wait_ge(elu_s, e * 2 + 2)
                nc.vector.scalar_tensor_tensor(out=ex[:, :, :], in0=ex[:, :, :], scalar=1.0, in1=rl[:, :, :],
                                               op0=ALU.min, op1=ALU.add).then_inc(elu_v, 1)

            def residual(e):
                dve.wait_ge(elu_v, e + 1)
                dve.wait_ge(xb_in[0], e * 16 + 16)
                dve.wait_ge(xn_free[0], e + 1)
                nc.vector.scalar_tensor_tensor(out=xn[:, :, :], in0=ex[:, :, :], scalar=-1.0, in1=xb[:, :, :],
                                               op0=ALU.add, op1=ALU.add).then_inc(xn_ready[0], 1)

            def new_statistics(e):
                dve.wait_ge(xn_ready[0], e + 1)
                statistics(1, lambda t: xn[:, t, :], 0, e + 1)

            def new_normalise(e, half):
                if half == 0:
                    dve.wait_ge(rstd_ready[1], e + 1)
                normalise(1, lambda t: xn[:, t, :], 0, half, e * 2 + half)

            def result(e):
                dve.wait_ge(acc_saved[1], e + 1)
                dve.wait_ge(xb_in[1], e * 16 + 16)
                dve.wait_ge(xn_free[1], e + 1)
                nc.vector.tensor_tensor(xn[:, :, :], hp[:, 0:BT, :], xb[:, :, :], ALU.add).then_inc(xn_ready[1], 1)

            dve.wait_ge(x_first, 16)
            with dve.Fori(0, NB // 2) as pair:
                def rows(side):
                    return lambda t: x_all[:, bass.ds(pair * 2 * BT + side * BT + t, 1), :].rearrange("p t f -> p (t f)")

                for side in range(2):
                    statistics(0, rows(side), side, pair * 2 + side + 1)
                for side in range(2):
                    dve.wait_ge(rstd_ready[0], pair * 2 + side + 1)
                    for half in range(2):
                        normalise(0, rows(side), side, half, pair * 4 + side * 2 + half)
                dve.wait_ge(x_rest, 16)
            scale_operands(0)

            def layer0_body(ib, cc, early=None, scale=None):
                body = ib * NCC + cc
                for k in range(BODY):
                    dve.wait_ge(evacuated, body * BODY + k + 1 + PT_SLOTS)
                    make_p(0, k, ib, cc, body * BODY + k)
                    if k < 2:
                        convert(2 + k, body * 16 + 16, body * BODY + ROW_SLOT_STEPS)
                    if k in (CT, CT + 1):
                        convert(k - CT, body * 16 + 32, body * BODY + CT + ROW_SLOT_STEPS)
                    if k == 2 and scale is not None:
                        scale_g(0, scale)
                    if early is not None:
                        at, e = early * BODY + k, ib - 1
                        if at == 2:
                            save_block(0, e)
                        if at == 6:
                            elu_sum(e)
                        if at == 7:
                            residual(e)
                        if at == 9:
                            new_statistics(e)
                        if at == 13 or at == 14:
                            new_normalise(e, at - 13)

            dve.wait_ge(q_first[0], 16)
            with dve.Fori(0, NCC - 1) as cc:
                layer0_body(0, cc, scale=cc + 1)
            layer0_body(0, NCC - 1)
            if NB > 1:
                dve.wait_ge(q_rest[0], 16)
            with dve.Fori(1, NB) as ib:
                for j in range(EARLY):
                    layer0_body(ib, j, early=j)
                with dve.Fori(EARLY, NCC) as cc:
                    layer0_body(ib, cc)
            e = NB - 1
            save_block(0, e)
            elu_sum(e)
            residual(e)
            new_statistics(e)
            for half in range(2):
                new_normalise(e, half)
            scale_operands(1)

            def layer1_body(ib, cc, early=False, scale=None):
                body = ib * NCC + cc
                for k in range(BODY):
                    if k % CT == 0:
                        dve.wait_ge(mask_in[k // CT], body * 16 + 16)
                    make_p(1, k, ib, cc, body * BODY + k)
                    if k == 2 and scale is not None:
                        scale_g(1, scale)
                    if early and k == 2:
                        save_block(1, ib - 1)
                    if early and k == 5:
                        result(ib - 1)

            dve.wait_ge(q_first[1], 16)
            with dve.Fori(0, NCC - 1) as cc:
                layer1_body(0, cc, scale=cc + 1)
            layer1_body(0, NCC - 1)
            if NB > 1:
                dve.wait_ge(q_rest[1], 16)
            with dve.Fori(1, NB) as ib:
                layer1_body(ib, 0, early=True)
                with dve.Fori(1, NCC) as cc:
                    layer1_body(ib, cc)
            save_block(1, NB - 1)
            result(NB - 1)

        @block.tensor
        def _(pe):
            pe.sem_inc(transposed, ROW_SLOT_STEPS)
            for l in L:
                pe.sem_inc(p_used[l], PR)
                pe.sem_inc(ht_pe[l], HID_SLOTS)
                pe.sem_inc(wh_ready[l], 2)
            pe.wait_ge(w_in, 64)
            pe.wait_ge(const_ready, 5)
            for l in L:
                if l:
                    pe.wait_ge(wprep_sb, 2)
                pe.transpose(bank[0][:, 0:P], wa[:, l, 0:F], ident[:, :]).then_inc(wprep_pe, 1)
                pe.wait_ge(wprep_sb, 2 * l + 1)
                pe.matmul(bank[1][:, 0:2], w_T[:, :], a_sb[:, l, :], start=True, stop=True).then_inc(wprep_pe, 1)
            pe.wait_ge(wprep_sb, 4)

            def transpose_half(l, unit, half, banks):
                pe.wait_ge(hid_ready[l], unit + 1)
                pe.wait_ge(ht_ready[l], unit + 1)
                for t in range(HR):
                    mm = pe.transpose(bank[banks[0]][:, t * P:(t + 1) * P], hid[:, half, t, :], ident[:, :])
                mm.then_inc(ht_pe[l], 1)

            def project_half(l, unit, half, banks):
                pe.wait_ge(ht_ready[l], unit + 1 + SETS[l])
                pe.wait_ge(wh_copied[l], unit + 1)
                for t in range(HR):
                    o = bank[banks[1 + t // 3]][:, (t % 3) * PW:(t % 3) * PW + PW]
                    mm = pe.matmul(o, hT[:, half, t * P:(t + 1) * P], wa[:, l, :], start=(t % 3 == 0), stop=True, skip_group_check=True)
                mm.then_inc(wh_ready[l], 1)

            def share(l):
                pe.wait_ge(mx_v[l], 1)
                pe.transpose(bank[7][0:1, 0:P], mx[:, 0:1], ident[:, :]).then_inc(mx_pe[l], 1)
                pe.wait_ge(mx_v[l], 2)
                pe.matmul(bank[6][:, 0:1], ones[0:1, :], mx[0:1, 1:2], start=True, stop=True).then_inc(mx_pe[l], 1)
                pe.wait_ge(hs_v[l], 2)
                pe.matmul(bank[5][:, 0:F], hs_rep[:, :], wa[:, l, 0:F], start=True, stop=True).then_inc(mx_pe[l], 1)
                pe.wait_ge(q_v[l], 1)
                pe.transpose(bank[7][0:NT, P:2 * P], qc_sb[:, :], ident[:, :]).then_inc(q_pe[l], 1)

            def transposes(k, pieces, step_ahead):
                if k % CT == 0:
                    pe.wait_ge(converted, pieces + ADJ_SLOTS)
                pe.wait_ge(evacuated, step_ahead + 1)
                for r in range(BT):
                    mm = pe.transpose(pt[k % 2][:, r * P:(r + 1) * P],
                                      row_sb[:, k // CT, r, (k % CT) * P:(k % CT + 1) * P], ident16[:, :])
                mm.then_inc(transposed, 1)

            def open_accumulators(l, ib):
                for k in range(BANKS):
                    pe.matmul(bank[k][:, 0:PER_BANK * GW], tiny16[:, :], mean16[:, :, :].rearrange("p t w -> p (t w)"),
                              start=True, stop=False, skip_group_check=True)

            def products(l, k, cc, step):
                pe.wait_ge(p_ready[l], step + 1 + COL_SLOTS)
                g = g_sb[l][:, bass.ds(cc * BODY + k, 1), 0:GW].rearrange("p t w -> p (t w)")
                for r in range(BT):
                    mm = pe.matmul(acc_tile(r), p_sb[:, k % PR, r * P:(r + 1) * P], g, start=False, stop=False,
                                   skip_group_check=True)
                mm.then_inc(p_used[l], 1)

            with pe.Fori(0, NB // 2) as pair:
                for k in range(4):
                    transpose_half(0, pair * 4 + k, k % 2, PROJECTION_BANKS[k % 2])
                    if k:
                        project_half(0, pair * 4 + k - 1, (k - 1) % 2, PROJECTION_BANKS[(k - 1) % 2])
                project_half(0, pair * 4 + 3, 1, PROJECTION_BANKS[1])
            share(0)
            for k in range(LEAD):
                transposes(k, 2, k)

            def layer0_body(ib, cc, early=None, scaled=False):
                body = ib * NCC + cc
                if scaled:
                    pe.wait_ge(g_ready[0], cc + 1)
                for k in range(BODY):
                    chunk = 2 * body + (k + LEAD) // CT
                    transposes((k + LEAD) % BODY, 2 * chunk + 2, body * BODY + k + LEAD)
                    products(0, k, cc, body * BODY + k)
                    if early is not None:
                        at, e = early * BODY + k, ib - 1
                        if at == 15 or at == 18:
                            project_half(1, e * 2 + (at - 15) // 3, (at - 15) // 3, PROJECTION_BANKS[0])
                        if at == 12 or at == 15:
                            transpose_half(1, e * 2 + (at - 12) // 3, (at - 12) // 3, PROJECTION_BANKS[0])

            pe.wait_ge(mean_s[0], 9)
            pe.wait_ge(f_placed[0], 1)
            open_accumulators(0, 0)
            with pe.Fori(0, NCC) as cc:
                layer0_body(0, cc, scaled=True)
            with pe.Fori(1, NB) as ib:
                pe.wait_ge(acc_saved[0], ib)
                open_accumulators(0, ib)
                for j in range(EARLY):
                    layer0_body(ib, j, early=j)
                with pe.Fori(EARLY, NCC) as cc:
                    layer0_body(ib, cc)
            e = NB - 1
            for half in range(2):
                transpose_half(1, e * 2 + half, half, PROJECTION_BANKS[0])
                project_half(1, e * 2 + half, half, PROJECTION_BANKS[0])
            share(1)

            def layer1_body(ib, cc, scaled=False):
                body = ib * NCC + cc
                if scaled:
                    pe.wait_ge(g_ready[1], cc + 1)
                for k in range(BODY):
                    products(1, k, cc, body * BODY + k)

            pe.wait_ge(mean_s[1], 9)
            pe.wait_ge(f_placed[1], 1)
            open_accumulators(1, 0)
            with pe.Fori(0, NCC) as cc:
                layer1_body(0, cc, scaled=True)
            with pe.Fori(1, NB) as ib:
                pe.wait_ge(acc_saved[1], ib)
                open_accumulators(1, ib)
                with pe.Fori(0, NCC) as cc:
                    layer1_body(ib, cc)


_INS = ['x', 'adj', 'L0_gnn_W', 'L0_gnn_a', 'L1_gnn_W', 'L1_gnn_a']
_OUTS = [((8192, 128), 'float32')]


def kernel(**inputs):
    import numpy as _np
    import concourse.bacc as _bacc
    from concourse import mybir as _mybir
    from concourse.bass_utils import run_bass_kernel_spmd as _run

    nc = _bacc.Bacc("TRN2", target_bir_lowering=False, num_devices=1)
    arrays, args = {}, []
    for name in _INS:
        a = _np.ascontiguousarray(inputs[name])
        arrays[f"in_{name}_dram"] = a
        args.append(nc.dram_tensor(f"in_{name}_dram", a.shape, _mybir.dt.from_np(a.dtype), kind="ExternalInput").ap())
    for i, (shape, dtype) in enumerate(_OUTS):
        dt = _mybir.dt.from_np(_np.dtype(dtype))
        args.append(nc.dram_tensor(f"out_{i}_dram", shape, dt, kind="ExternalOutput").ap())
    gat_two_layers(nc, *args)
    r = _run(nc, [arrays], core_ids=[0])
    got = tuple(r.results[0][f"out_{i}_dram"] for i in range(len(_OUTS)))
    return got[0]
```

```python
from contextlib import ExitStack

import concourse.bass as bass
from concourse import mybir

ALU = mybir.AluOpType
ACT = mybir.ActivationFunctionType
AX_X = mybir.AxisListType.X
F32 = mybir.dt.float32
BF16 = mybir.dt.bfloat16
I8 = mybir.dt.int8
I32 = mybir.dt.int32

P = 128
SLOPE = 0.2
EPS = 1e-5


def gat_two_layers(nc, x, adj, w0, a0, w1, a1, out):
    N, F = x.shape
    NT = N // P
    BT = 8
    BI = BT * P
    NB = NT // BT
    CT = 4
    CJ = CT * P
    BODY = 2 * CT
    NCC = NT // BODY
    EARLY = 5
    GW = F + 1
    PW = F + 2
    PER_BANK = 3
    BANKS = 3
    SLOTS = BANKS * PER_BANK
    PAIRS = BODY // 2
    AHEAD = 2
    PR = 4
    HR = BT // 2
    UNITS = NT // HR
    ONE = -64
    TINY = 2.0 ** -100

    ctx = ExitStack()
    with ctx:
        def sb(name, shape, dt=F32):
            return ctx.enter_context(nc.sbuf_tensor(name, shape, dt))

        def sem(name):
            return ctx.enter_context(nc.semaphore(name))

        g_sb = [sb(f"g{l}_sb", [P, NT, PW]) for l in range(2)]
        q_sb = sb("q_sb", [P, N])
        x_all = q_sb[:, :].rearrange("p (t f) -> p t f", f=F)
        adj_sb = sb("adj_sb", [P, 4, HR, CJ], I32)
        row_sb = sb("row_sb", [P, 2, BT, CJ // 2], BF16)
        col_sb = sb("col_sb", [P, 2, CT // 2, BI], BF16)
        p_sb = sb("p_sb", [P, PR, BI])
        hp = sb("hp", [P, SLOTS, GW])
        xb = sb("xb", [P, BT, F])
        xn = sb("xn", [P, BT, F])
        ex = sb("ex", [P, BT, F])
        rl = sb("rl", [P, BT, F])
        hid = sb("hid", [P, 2, HR, F])
        hT = sb("hT", [P, 2, HR * P])
        rec = sb("rec", [P, SLOTS])
        bn = sb("bn", [P, 2 * BT, 6])
        mv = sb("mv", [P, 2 * BT, 2])
        ve = sb("ve", [P, 2 * BT])
        rstd = sb("rstd", [P, 2 * BT])
        scale_s = sb("scale_s", [P, HR])
        shift_s = sb("shift_s", [P, HR])
        mhalf = sb("mhalf", [P, BT])
        t_sb = sb("t_sb", [P, NT])
        f_sb = sb("f_sb", [P, NT])
        qc_sb = sb("qc_sb", [P, NT])
        qT_sb = sb("qT_sb", [P, P])
        wa = sb("wa", [P, 2, PW])
        w_T = sb("w_T", [P, P])
        a_sb = sb("a_sb", [P, 2, 2])
        ident = sb("ident", [P, P])
        ident16 = sb("ident16", [P, P], BF16)
        ones = sb("ones", [P, P])
        tiny16 = sb("tiny16", [P, P], BF16)
        tiny = sb("tiny", [P, P])
        hsum = sb("hsum", [P, UNITS])
        hs = sb("hs", [P, 1])
        hs_rep = sb("hs_rep", [P, P])
        mean_v = sb("mean_v", [P, PER_BANK, GW])
        m_hi = sb("m_hi", [P, GW], BF16)
        m_mid = sb("m_mid", [P, GW], BF16)
        rest1 = sb("rest1", [P, GW])
        rest2 = sb("rest2", [P, GW])
        mean16 = sb("mean16", [P, PER_BANK, GW], BF16)
        mx = sb("mx", [P, 4])

        psum = ctx.enter_context(nc.psum_tensor("psum", [P, 8, 512], F32))
        bank = [psum[:, i, :] for i in range(8)]
        pt = [bank[3].bitcast(BF16), bank[4].bitcast(BF16)]
        PROJECTION_BANKS = [(5, 6, 7), (2, 0, 1)]
        SETS = [2, 1]

        mask_dram = nc.dram_tensor("mask_cols", [NB, NCC * 2, P, CT // 2 * BI], BF16, kind="Internal").ap()
        x1_dram = nc.dram_tensor("x1_rows", [NB, P, BT, F], F32, kind="Internal").ap()
        q_dram = [nc.dram_tensor(f"q_row{l}", [NT, P], F32, kind="Internal").ap() for l in range(2)]

        def acc_tile(r):
            return bank[r // PER_BANK][:, (r % PER_BANK) * GW:(r % PER_BANK) * GW + GW]

        L = range(2)
        x_first, x_second, x_third, x_rest, w_in = (sem(n) for n in ("x_first", "x_second", "x_third", "x_rest", "w_in"))
        const_ready, half_ready, col_zeroed = sem("const_ready"), sem("half_ready"), sem("col_zeroed")
        wprep_pe, wprep_sb = sem("wprep_pe"), sem("wprep_sb")
        adj_in = [sem(f"adj_in{i}") for i in range(4)]
        converted = sem("converted")
        transposed = sem("transposed")
        evacuated = sem("evacuated")
        stored = [sem(f"stored{i}") for i in range(2)]
        mask_in = [sem(f"mask_in{i}") for i in range(2)]
        p_ready = [sem(f"p_ready{l}") for l in L]
        p_used = [sem(f"p_used{l}") for l in L]
        rec_done = [sem(f"rec_done{l}") for l in L]
        bank_done = [[sem(f"bank{k}_done{l}") for k in range(BANKS - 1)] for l in L]
        acc_copied = [sem(f"acc_copied{l}") for l in L]
        acc_saved = [sem(f"acc_saved{l}") for l in L]
        xb_in = [sem(f"xb_in{l}") for l in L]
        elu_s, elu_v, xn_ready = sem("elu_s"), sem("elu_v"), [sem(f"xn_ready{l}") for l in L]
        xn_out = [sem(f"xn_out{l}") for l in L]
        xn_free = [sem(f"xn_free{l}") for l in L]
        stats_v = [sem(f"stats_v{l}") for l in L]
        parts_seen = sem("parts_seen")
        stats_done = [sem(f"stats_done{l}") for l in L]
        eps_added = [sem(f"eps_added{l}") for l in L]
        rstd_ready = [sem(f"rstd_ready{l}") for l in L]
        hid_ready = [sem(f"hid_ready{l}") for l in L]
        ht_pe = [sem(f"ht_pe{l}") for l in L]
        ht_ready = [sem(f"ht_ready{l}") for l in L]
        wh_ready = [sem(f"wh_ready{l}") for l in L]
        wh_copied = [sem(f"wh_copied{l}") for l in L]
        mx_v, mx_pe = [sem(f"mx_v{l}") for l in L], [sem(f"mx_pe{l}") for l in L]
        hs_v = [sem(f"hs_v{l}") for l in L]
        exps = [sem(f"exps{l}") for l in L]
        q_v = [sem(f"q_v{l}") for l in L]
        q_pe = [sem(f"q_pe{l}") for l in L]
        q_out, q_rest = ([sem(f"{n}{l}") for l in L] for n in ("q_out", "q_rest"))
        q_row_pe = [sem(f"q_row_pe{l}") for l in L]
        q_row_s = [sem(f"q_row_s{l}") for l in L]
        q_row_v = [sem(f"q_row_v{l}") for l in L]
        mean_p = [sem(f"mean_p{l}") for l in L]
        affine_ready, hid_ready_s = sem("affine_ready"), sem("hid_ready_s")
        last_saved, last_elu, last_sum, last_xn = (sem(n) for n in ("last_saved", "last_elu", "last_sum", "last_xn"))
        last_parts, last_stats, last_eps, last_rstd = (sem(n) for n in ("last_parts", "last_stats", "last_eps", "last_rstd"))
        f_placed = [sem(f"f_placed{l}") for l in L]
        g_ready = [sem(f"g_ready{l}") for l in L]
        mean_s = [sem(f"mean_s{l}") for l in L]

        ADJ_SLOTS, ROW_SLOT_PAIRS, PT_SLOTS, COL_SLOTS, HID_SLOTS = 4, CT // 2, 2, BODY, 2

        x_v = x.rearrange("(b m p s) f -> b p m (s f)", p=P, s=2, m=BT // 2)
        xt_v = x.rearrange("(m p s) f -> p m (s f)", p=P, s=2)
        out_v = out.rearrange("(b m p s) f -> b p m (s f)", p=P, s=2, m=BT // 2)
        adj_v = adj.rearrange("(b h m p s) (c j) -> b h m p s c j", p=P, s=2, m=HR // 2, h=2, c=NCC * 2)

        def in_pairs(rows):
            return rows.rearrange("p (m s) f -> p m (s f)", s=2)

        block = ctx.enter_context(nc.Block())

        @block.sync
        def _(sp):
            FIRST = 2 * BT
            sp.dma_start(in_pairs(x_all[:, 0:BT, :]), xt_v[:, 0:BT // 2, :]).then_inc(x_first, 16)
            sp.dma_start(in_pairs(x_all[:, BT:FIRST, :]), xt_v[:, BT // 2:FIRST // 2, :]).then_inc(x_second, 16)
            for l, (w, a) in enumerate(((w0, a0), (w1, a1))):
                sp.dma_start(wa[:, l, 0:F], w).then_inc(w_in, 16)
                with nc.allow_non_contiguous_dma(reason="256 score weights, once"):
                    sp.dma_start(a_sb[:, l, :], a.rearrange("(k f) o -> f (k o)", k=2)).then_inc(w_in, 16)
            sp.dma_start(in_pairs(x_all[:, FIRST:2 * FIRST, :]), xt_v[:, FIRST // 2:FIRST, :]).then_inc(x_third, 16)
            sp.dma_start(in_pairs(x_all[:, 2 * FIRST:NT, :]), xt_v[:, FIRST:NT // 2, :]).then_inc(x_rest, 16)
            with sp.Fori(0, NB) as ib:
                with sp.Fori(0, NCC) as cc:
                    body = ib * NCC + cc
                    for slot in range(ADJ_SLOTS):
                        ch, half = slot // 2, slot % 2
                        sp.wait_ge(converted, body * 4 + slot + 1)
                        for m in range(HR // 2):
                            src = adj_v[bass.ds(ib, 1), half, m, :, :, bass.ds(cc * 2 + ch, 1), :]
                            sp.dma_start(adj_sb[:, slot, 2 * m:2 * m + 2, :], src.rearrange("a p s c j -> p (a s) (c j)")).then_inc(adj_in[slot], 16)
            for slot in range(ADJ_SLOTS):
                sp.wait_ge(converted, NB * NCC * 4 + slot + 1)
                for m in range(HR // 2):
                    sp.dma_start(adj_sb[:, slot, 2 * m:2 * m + 2, :], adj_v[0, slot % 2, m, :, :, slot // 2, :]).then_inc(adj_in[slot], 16)
            for ch in range(2):
                sp.wait_ge(stored[ch], 16 * (NB * NCC + 1))
            sp.wait_ge(p_ready[0], NB * NT + COL_SLOTS)
            sp.wait_ge(evacuated, NB * NT // 2 + 1 + PT_SLOTS)
            with sp.Fori(0, NB) as ib:
                with sp.Fori(0, NCC) as cc:
                    body = ib * NCC + cc
                    for ch in range(2):
                        sp.wait_ge(p_ready[1], body * BODY + ch * CT + CT)
                        src = mask_dram[bass.ds(ib, 1), bass.ds(cc * 2 + ch, 1), :, :]
                        sp.dma_start(col_sb[:, ch, :, :], src.rearrange("a c p (d i) -> p (a c d) i", d=CT // 2)).then_inc(mask_in[ch], 16)

        @block.gpsimd
        def _(pool):
            nc.gpsimd.memset(mhalf[:, :], -0.5).then_inc(half_ready, 1)
            nc.gpsimd.memset(ident[:, :], 0.0).then_inc(const_ready, 1)
            nc.gpsimd.memset(ones[:, :], 1.0).then_inc(const_ready, 1)
            nc.gpsimd.memset(tiny16[:, :], ONE * TINY).then_inc(const_ready, 1)
            pool.wait_ge(half_ready, 1)
            pool.wait_ge(const_ready, 3)
            nc.gpsimd.affine_select(out=ident[:, :], in_=ident[:, :], compare_op=ALU.not_equal, fill=1.0, base=0,
                                    pattern=[[-1, P]], channel_multiplier=1).then_inc(const_ready, 1)
            pool.wait_ge(const_ready, 4)
            nc.gpsimd.tensor_copy(ident16[:, :], ident[:, :]).then_inc(const_ready, 1)
            nc.gpsimd.memset(tiny[:, :], 0.0).then_inc(half_ready, 1)
            nc.gpsimd.memset(qT_sb[:, :], 0.0).then_inc(half_ready, 1)
            pool.wait_ge(half_ready, 3)
            nc.gpsimd.memset(tiny[0:1, :], ONE * TINY).then_inc(const_ready, 1)
            nc.gpsimd.memset(mean_v[:, :, F:GW], 1.0).then_inc(const_ready, 1)
            nc.gpsimd.memset(mean16[:, :, :], 0.0).then_inc(const_ready, 1)
            pool.wait_ge(const_ready, 8)
            pool.sem_inc(xn_free[0], 1)

            def inverse_deviation(l, side, count):
                s = slice(side * BT, side * BT + BT)
                pool.wait_ge(eps_added[l], count)
                nc.gpsimd.tensor_tensor(rstd[:, s], ve[:, s], mhalf[:, :], ALU.pow).then_inc(rstd_ready[l], 1)

            def split_mean(l):
                m = mean_v[:, 0, :]
                pool.wait_ge(mean_s[l], 1)
                nc.gpsimd.tensor_copy(m_hi[:, :], m).then_inc(mean_p[l], 1)
                pool.wait_ge(mean_p[l], 1)
                nc.gpsimd.tensor_tensor(rest1[:, :], m, m_hi[:, :], ALU.subtract).then_inc(mean_p[l], 1)
                pool.wait_ge(mean_p[l], 2)
                nc.gpsimd.tensor_copy(m_mid[:, :], rest1[:, :]).then_inc(mean_p[l], 1)
                pool.wait_ge(mean_p[l], 3)
                nc.gpsimd.tensor_tensor(rest2[:, :], rest1[:, :], m_mid[:, :], ALU.subtract).then_inc(mean_p[l], 1)
                pool.wait_ge(mean_p[l], 4)
                for part, src in enumerate((m_hi, m_mid, rest2)):
                    row = slice(32 * part, 32 * part + 1)
                    for k in range(PER_BANK):
                        ins = nc.gpsimd.tensor_copy(mean16[row, k, :], src[row, :])
                ins.then_inc(mean_p[l], 1)

            def spread_q(l):
                pool.wait_ge(q_v[l], 2)
                pool.dma_start(q_dram[l], qT_sb[0:NT, :]).then_inc(q_out[l], 16)
                pool.wait_ge(q_out[l], 16)
                row = q_dram[l].rearrange("t p -> (t p)")
                if NB > 1:
                    pool.dma_start(q_sb[:, BI:N], row[BI:N].partition_broadcast(P)).then_inc(q_rest[l], 16)
                split_mean(l)

            with pool.Fori(0, NB // 2) as pair:
                for side in range(2):
                    inverse_deviation(0, side, pair * 2 + side + 1)
            spread_q(0)
            with pool.Fori(0, NB - 1) as e:
                pool.dma_start(in_pairs(xb[:, :, :]), x_v[bass.ds(e, 1)].rearrange("a p m f -> p (a m) f")).then_inc(xb_in[0], 16)
                inverse_deviation(1, 0, e + 1)
                pool.dma_start(x1_dram[bass.ds(e, 1)].rearrange("a p t f -> p (a t) f"), xn[:, :, :]).then_inc(xn_out[0], 16)
                pool.wait_ge(xn_out[0], e * 16 + 16)
                pool.sem_inc(xn_free[0], 1)
            pool.dma_start(in_pairs(xb[:, :, :]), x_v[NB - 1]).then_inc(xb_in[0], 16)
            for half in range(2):
                s = slice(half * HR, half * HR + HR)
                pool.wait_ge(last_eps, half + 1)
                nc.gpsimd.tensor_tensor(rstd[:, s], ve[:, s], mhalf[:, s], ALU.pow).then_inc(last_rstd, 1)
            pool.dma_start(x1_dram[NB - 1], xn[:, :, :]).then_inc(xn_out[0], 16)
            spread_q(1)

        @block.scalar
        def _(act):
            act.sem_inc(evacuated, PT_SLOTS)
            for l in L:
                act.sem_inc(ht_ready[l], SETS[l])
                act.sem_inc(wh_copied[l], SETS[l])
            act.wait_ge(col_zeroed, 1)
            for ch in range(2):
                act.dma_start(mask_dram[NB - 1, 2 * NCC - 2 + ch], col_sb[:, ch, :, :].rearrange("p d i -> p (d i)")).then_inc(stored[ch], 16)
            for l in L:
                act.wait_ge(wprep_pe, 2 * l + 1)
                nc.scalar.activation(w_T[:, :], bank[0][:, 0:P], ACT.Copy).then_inc(wprep_sb, 1)
                act.wait_ge(wprep_pe, 2 * l + 2)
                nc.scalar.activation(wa[:, l, F:PW], bank[1][:, 0:2], ACT.Copy).then_inc(wprep_sb, 1)

            def relu_half(l, unit, half, banks):
                act.wait_ge(ht_pe[l], unit + 1 + HID_SLOTS)
                act.wait_ge(wh_ready[l], unit + 1)
                nc.scalar.activation(hT[:, half, :], bank[banks[0]], ACT.Relu,
                                     accum_out=hsum[:, bass.ds(unit, 1)]).then_inc(ht_ready[l], 1)

            def copy_projection(l, unit, banks):
                act.wait_ge(wh_ready[l], unit + 1 + 2)
                g = g_sb[l]
                nc.scalar.activation(g[:, bass.ds(unit * HR, 3), :], bank[banks[1]][:, 0:3 * PW].rearrange("p (t w) -> p t w", w=PW), ACT.Copy)
                nc.scalar.activation(g[:, bass.ds(unit * HR + 3, 1), :], bank[banks[2]][:, 0:PW].rearrange("p (t w) -> p t w", w=PW),
                                     ACT.Copy).then_inc(wh_copied[l], 1)

            def exponentials(l):
                s1 = g_sb[l][:, :, F:F + 1].rearrange("p t o -> p (t o)")
                s2 = g_sb[l][:, :, F + 1:PW].rearrange("p t o -> p (t o)")
                act.wait_ge(mx_v[l], 4)
                nc.scalar.activation(qc_sb[:, :], s1, ACT.Exp, bias=mx[:, 2:3], scale=-(1 - SLOPE)).then_inc(exps[l], 1)
                nc.scalar.activation(f_sb[:, :], s2, ACT.Exp, bias=mx[:, 3:4], scale=SLOPE).then_inc(exps[l], 1)
                nc.scalar.activation(t_sb[:, :], s2, ACT.Exp, bias=mx[:, 2:3], scale=1 - SLOPE).then_inc(exps[l], 1)
                act.wait_ge(mx_pe[l], 3)
                for k in range(PER_BANK):
                    ins = nc.scalar.activation(mean_v[:, k, 0:F], bank[2][:, 0:F], ACT.Copy)
                ins.then_inc(mean_s[l], 1)
                act.wait_ge(q_row_pe[l], 2)
                nc.scalar.activation(q_sb[:, HR * P:BI], bank[6], ACT.Copy).then_inc(q_row_s[l], 1)

            with act.Fori(0, NB // 2) as pair:
                def normalise_last():
                    act.wait_ge(affine_ready, pair + 1)
                    act.wait_ge(ht_pe[0], pair * 4 + 3 + 1)
                    for t in range(HR):
                        rows = x_all[:, bass.ds(pair * 2 * BT + BT + HR + t, 1), :].rearrange("p t f -> p (t f)")
                        ins = nc.scalar.activation(hid[:, 1, t, :], rows, ACT.Identity, bias=shift_s[:, t:t + 1], scale=scale_s[:, t:t + 1])
                    ins.then_inc(hid_ready_s, 1)

                def relu(k):
                    relu_half(0, pair * 4 + k, k % 2, PROJECTION_BANKS[k % 2])

                def copy(k):
                    copy_projection(0, pair * 4 + k, PROJECTION_BANKS[k % 2])

                relu(0)
                relu(1)
                copy(0)
                normalise_last()
                copy(1)
                relu(2)
                relu(3)
                copy(2)
                copy(3)

            def evacuate(q, pair):
                act.wait_ge(transposed, pair + 1 + ROW_SLOT_PAIRS)
                act.wait_ge(p_ready[0], pair * 2 + 2)
                nc.scalar.activation(col_sb[:, q // 2, q % 2, :], pt[q % 2], ACT.Copy).then_inc(evacuated, 1)

            def store(ch, ib, cc, pairs_done):
                act.wait_ge(evacuated, pairs_done + PT_SLOTS)
                dst = mask_dram[bass.ds(ib, 1), bass.ds(cc * 2 + ch, 1), :, :].rearrange("a c p w -> p (a c w)")
                act.dma_start(dst, col_sb[:, ch, :, :].rearrange("p d i -> p (d i)")).then_inc(stored[ch], 16)

            def copy_accumulators(l, e):
                for k in range(BANKS):
                    if k < BANKS - 1:
                        act.wait_ge(bank_done[l][k], e * NT + NT)
                    else:
                        act.wait_ge(p_used[l], e * NT + NT + PR)
                    nc.scalar.activation(hp[:, k * PER_BANK:(k + 1) * PER_BANK, :].rearrange("p t w -> p (t w)"),
                                         bank[k][:, 0:PER_BANK * GW], ACT.Copy).then_inc(acc_copied[l], 1)

            def elu_parts(e, part):
                act.wait_ge(acc_saved[0], e + 1)
                o, fn = ((ex, ACT.Exp), (rl, ACT.Relu))[part]
                nc.scalar.activation(o[:, :, :], hp[:, 0:BT, 0:F], fn).then_inc(elu_s, 1)

            def masks_out(ib, cc, early=None):
                body = ib * NCC + cc
                for k in range(BODY):
                    if k % 2 == 0:
                        q = k // 2 + 1
                        if q == PAIRS // 2:
                            act.wait_ge(stored[1], body * 16 + 16)
                        if q == PAIRS:
                            act.wait_ge(stored[0], body * 16 + 32)
                        evacuate(q % PAIRS, body * PAIRS + q)
                    if k == 0:
                        store(0, ib, cc, body * PAIRS + PAIRS // 2)
                    if k == CT:
                        store(1, ib, cc, body * PAIRS + PAIRS)
                    if early is not None:
                        at, e = early * BODY + k, ib - 1
                        if at == 1:
                            copy_accumulators(0, e)
                        if at == 3 or at == 4:
                            elu_parts(e, at - 3)
                        if at == 34 or at == 38:
                            copy_projection(1, e * 2 + (at - 34) // 4, PROJECTION_BANKS[0])
                        if at == 30 or at == 34:
                            relu_half(1, e * 2 + (at - 30) // 4, (at - 30) // 4, PROJECTION_BANKS[0])

            act.wait_ge(stored[0], 16)
            evacuate(0, 0)
            exponentials(0)
            with act.Fori(0, NCC) as cc:
                masks_out(0, cc)
            with act.Fori(1, NB) as ib:
                for j in range(EARLY):
                    masks_out(ib, j, early=j)
                with act.Fori(EARLY, NCC) as cc:
                    masks_out(ib, cc)
            e = NB - 1
            copy_accumulators(0, e)
            for half in range(2):
                act.wait_ge(last_saved, half + 1)
                for o, fn in ((ex, ACT.Exp), (rl, ACT.Relu)):
                    nc.scalar.activation(o[:, half * HR:(half + 1) * HR, :], hp[:, half * HR:(half + 1) * HR, 0:F], fn).then_inc(last_elu, 1)
            for half in range(2):
                relu_half(1, e * 2 + half, half, PROJECTION_BANKS[0])
                copy_projection(1, e * 2 + half, PROJECTION_BANKS[0])
            exponentials(1)

            act.wait_ge(xn_out[0], 16 * NB)
            act.sem_inc(xn_free[1], 1)
            act.dma_start(xb[:, :, :], x1_dram[0]).then_inc(xb_in[1], 16)
            with act.Fori(0, NB - 1) as e:
                copy_accumulators(1, e)
                act.wait_ge(xn_ready[1], e + 1)
                act.dma_start(out_v[bass.ds(e, 1)].rearrange("a p m f -> p (a m) f"), in_pairs(xn[:, :, :])).then_inc(xn_out[1], 16)
                act.dma_start(xb[:, :, :], x1_dram[bass.ds(e + 1, 1)].rearrange("a p t f -> p (a t) f")).then_inc(xb_in[1], 16)
                act.wait_ge(xn_out[1], e * 16 + 16)
                act.sem_inc(xn_free[1], 1)
            copy_accumulators(1, NB - 1)
            for half in range(2):
                act.wait_ge(xn_ready[1], NB + half)
                act.dma_start(out_v[NB - 1, :, half * HR // 2:(half + 1) * HR // 2, :],
                              in_pairs(xn[:, half * HR:(half + 1) * HR, :])).then_inc(xn_out[1], 16)
            act.wait_ge(xn_out[1], 16 * (NB + 1))

        @block.vector
        def _(dve):
            nc.vector.memset(col_sb[:, :, :, :].bitcast(F32), 0.0).then_inc(col_zeroed, 1)
            dve.sem_inc(converted, ADJ_SLOTS)
            for l in L:
                dve.sem_inc(p_ready[l], COL_SLOTS)

            def partial_statistics(l, src, side, tiles):
                for t in tiles:
                    ins = nc.vector.bn_stats(bn[:, side * BT + t, :], src(t))
                if t == BT - 1:
                    ins.then_inc(stats_v[l], 1)

            def statistics(l, side, count):
                dve.wait_ge(stats_v[l], count)
                dve.sem_inc(parts_seen, 1)
                for t in range(BT):
                    ins = nc.vector.bn_aggr(mv[:, side * BT + t, :], bn[:, side * BT + t, :])
                ins.then_inc(stats_done[l], 1)
                add_eps(side * BT, BT, stats_done[l], count).then_inc(eps_added[l], 1)

            def add_eps(first, tiles, done, count):
                s = slice(first, first + tiles)
                dve.wait_ge(done, count)
                return nc.vector.tensor_scalar(ve[:, s], mv[:, s, 1:2].rearrange("p t o -> p (t o)"), EPS, None, ALU.add)

            def normalise(l, src, side, half, unit):
                dve.wait_ge(ht_pe[l], unit + 1)
                for t in range(HR):
                    i = side * BT + half * HR + t
                    ins = nc.vector.tensor_scalar(hid[:, half, t, :], src(half * HR + t), mv[:, i, 0:1], rstd[:, i:i + 1],
                                                  ALU.subtract, ALU.mult)
                ins.then_inc(hid_ready[l], 1)

            def convert(slot, value, chunk_free=None):
                dve.wait_ge(adj_in[slot], value)
                if chunk_free is not None:
                    dve.wait_ge(transposed, chunk_free)
                half = slot % 2
                nc.vector.tensor_scalar(row_sb[:, slot // 2, half * HR:(half + 1) * HR, :].bitcast(I8), adj_sb[:, slot, :, :], 0, ONE,
                                        ALU.is_gt, ALU.mult).then_inc(converted, 1)

            def scale_operands(l):
                g = g_sb[l]
                s2 = g[:, :, F + 1:PW].rearrange("p t o -> p (t o)")
                dve.wait_ge(wh_copied[l], UNITS + SETS[l])
                nc.vector.tensor_reduce(mx[:, 0:1], s2, AX_X, ALU.max).then_inc(mx_v[l], 1)
                nc.vector.tensor_reduce(hs[:, :], hsum[:, :], AX_X, ALU.add).then_inc(hs_v[l], 1)
                dve.wait_ge(mx_pe[l], 1)
                nc.vector.tensor_reduce(mx[0:1, 1:2], bank[7][0:1, 0:P], AX_X, ALU.max).then_inc(mx_v[l], 1)
                dve.wait_ge(mx_pe[l], 2)
                nc.vector.tensor_scalar(mx[:, 2:3], bank[6][:, 0:1], -(1 - SLOPE), None, ALU.mult).then_inc(mx_v[l], 1)
                nc.vector.tensor_scalar(mx[:, 3:4], bank[6][:, 0:1], -SLOPE, None, ALU.mult).then_inc(mx_v[l], 1)
                dve.wait_ge(hs_v[l], 1)
                nc.vector.tensor_scalar(hs_rep[:, :], ones[:, :], hs[:, 0:1], 1.0 / N, ALU.mult, ALU.mult).then_inc(hs_v[l], 1)
                dve.wait_ge(exps[l], 1)
                nc.vector.tensor_scalar(qc_sb[:, :], qc_sb[:, :], 1.0, None, ALU.min).then_inc(q_v[l], 1)
                dve.wait_ge(q_pe[l], 1)
                nc.vector.tensor_copy(qT_sb[0:NT, :], bank[7][0:NT, P:2 * P]).then_inc(q_v[l], 1)
                dve.wait_ge(exps[l], 3)
                nc.vector.tensor_copy(g[:, :, F:GW].rearrange("p t o -> p (t o)"), f_sb[:, :]).then_inc(f_placed[l], 1)
                scale_g(l, 0)
                dve.wait_ge(q_row_pe[l], 1)
                nc.vector.tensor_copy(q_sb[:, 0:HR * P], bank[5]).then_inc(q_row_v[l], 1)
                dve.wait_ge(q_row_v[l], 1)
                dve.wait_ge(q_row_s[l], 1)

            def scale_g(l, part):
                tiles = bass.ds(part * BODY, BODY)
                g = g_sb[l][:, tiles, 0:F]
                nc.vector.tensor_tensor(g, g, f_sb[:, tiles].to_broadcast([P, BODY, F]), ALU.mult).then_inc(g_ready[l], 1)

            def make_p(l, k, ib, cc, step):
                mask = col_sb[:, k // CT, k % CT // 2, :].bitcast(I8).rearrange("p (i s) -> p i s", s=2)[:, :, k % 2]
                dve.wait_ge(p_used[l], step + 1)
                nc.vector.scalar_tensor_tensor(out=p_sb[:, k % PR, :], in0=q_sb[:, bass.ds(ib * BI, BI)],
                                               scalar=t_sb[:, bass.ds(cc * BODY + k, 1)], in1=mask,
                                               op0=ALU.max, op1=ALU.mult).then_inc(p_ready[l], 1)

            def save_block(l, e):
                dve.wait_ge(acc_copied[l], e * BANKS + BANKS)
                nc.vector.reciprocal(rec[:, :], hp[:, :, F:GW].rearrange("p t o -> p (t o)")).then_inc(rec_done[l], 1)
                dve.wait_ge(rec_done[l], e + 1)
                nc.vector.tensor_tensor(hp[:, :, 0:F], hp[:, :, 0:F], rec[:, :].to_broadcast([P, SLOTS, F]),
                                        ALU.mult).then_inc(acc_saved[l], 1)

            def elu_sum(e):
                dve.wait_ge(elu_s, e * 2 + 2)
                nc.vector.scalar_tensor_tensor(out=ex[:, :, :], in0=ex[:, :, :], scalar=1.0, in1=rl[:, :, :],
                                               op0=ALU.min, op1=ALU.add).then_inc(elu_v, 1)

            def residual(e):
                dve.wait_ge(elu_v, e + 1)
                dve.wait_ge(xb_in[0], e * 16 + 16)
                dve.wait_ge(xn_free[0], e + 1)
                nc.vector.scalar_tensor_tensor(out=xn[:, :, :], in0=ex[:, :, :], scalar=-1.0, in1=xb[:, :, :],
                                               op0=ALU.add, op1=ALU.add).then_inc(xn_ready[0], 1)

            def new_partial_statistics(e, tiles):
                if 0 in tiles:
                    dve.wait_ge(xn_ready[0], e + 1)
                partial_statistics(1, lambda t: xn[:, t, :], 0, tiles)

            def new_normalise(e, half):
                if half == 0:
                    dve.wait_ge(rstd_ready[1], e + 1)
                normalise(1, lambda t: xn[:, t, :], 0, half, e * 2 + half)

            def result(e):
                dve.wait_ge(acc_saved[1], e + 1)
                dve.wait_ge(xb_in[1], e * 16 + 16)
                dve.wait_ge(xn_free[1], e + 1)
                nc.vector.tensor_tensor(xn[:, :, :], hp[:, 0:BT, 0:F], xb[:, :, :], ALU.add).then_inc(xn_ready[1], 1)

            def before_layer0(pair):
                def rows(side):
                    return lambda t: x_all[:, bass.ds(pair * 2 * BT + side * BT + t, 1), :].rearrange("p t f -> p (t f)")

                for side in range(2):
                    partial_statistics(0, rows(side), side, range(BT))
                    statistics(0, side, pair * 2 + side + 1)
                    if side == 0:
                        dve.wait_ge(x_second, 16)
                dve.wait_ge(rstd_ready[0], pair * 2 + 1)
                for half in range(2):
                    normalise(0, rows(0), 0, half, pair * 4 + half)
                dve.wait_ge(rstd_ready[0], pair * 2 + 2)
                dve.wait_ge(ht_pe[0], pair * 4 + HID_SLOTS)
                s = slice(BT + HR, 2 * BT)
                nc.vector.tensor_copy(scale_s[:, :], rstd[:, s])
                nc.vector.scalar_tensor_tensor(out=shift_s[:, :], in0=mv[:, s, 0:1].rearrange("p t o -> p (t o)"), scalar=-1.0,
                                               in1=rstd[:, s], op0=ALU.mult, op1=ALU.mult).then_inc(affine_ready, 1)
                normalise(0, rows(1), 1, 0, pair * 4 + 2)

            dve.wait_ge(x_first, 16)
            with dve.Fori(0, 2) as pair:
                before_layer0(pair)
                dve.wait_ge(x_third, 16)
            dve.wait_ge(x_rest, 16)
            with dve.Fori(2, NB // 2) as pair:
                before_layer0(pair)
            for slot in range(ADJ_SLOTS):
                convert(slot, 32)
            scale_operands(0)

            def layer0_body(ib, cc, early=None, scale=None):
                body = ib * NCC + cc
                for k in range(BODY):
                    if k % 2 == 0:
                        dve.wait_ge(evacuated, body * PAIRS + k // 2 + 1 + PT_SLOTS)
                    make_p(0, k, ib, cc, body * BODY + k)
                    if k % CT >= 2:
                        ch = k // CT
                        convert(2 * ch + k % 2, body * 32 + 64, body * PAIRS + (ch + 1) * PAIRS // 2 + ROW_SLOT_PAIRS)
                    if k == 4 and scale is not None:
                        scale_g(0, scale)
                    if early is not None:
                        at, e = early * BODY + k, ib - 1
                        if at == 4:
                            save_block(0, e)
                        if at == 9:
                            elu_sum(e)
                        if at == 13:
                            residual(e)
                        if 16 <= at < 16 + BT:
                            new_partial_statistics(e, range(at - 16, at - 15))
                        if at == 16 + BT:
                            statistics(1, 0, e + 1)
                        if at == 27 or at == 30:
                            new_normalise(e, (at - 27) // 3)

            with dve.Fori(0, NCC - 1) as cc:
                layer0_body(0, cc, scale=cc + 1)
            layer0_body(0, NCC - 1)
            if NB > 1:
                dve.wait_ge(q_rest[0], 16)
            with dve.Fori(1, NB) as ib:
                for j in range(EARLY):
                    layer0_body(ib, j, early=j)
                with dve.Fori(EARLY, NCC) as cc:
                    layer0_body(ib, cc)
            e = NB - 1
            dve.wait_ge(acc_copied[0], NB * BANKS)
            nc.vector.reciprocal(rec[:, :], hp[:, :, F:GW].rearrange("p t o -> p (t o)")).then_inc(rec_done[0], 1)
            dve.wait_ge(rec_done[0], NB)
            halves = [slice(half * HR, half * HR + HR) for half in range(2)]
            for t in halves:
                nc.vector.tensor_tensor(hp[:, t, 0:F], hp[:, t, 0:F], rec[:, t].to_broadcast([P, HR, F]), ALU.mult).then_inc(last_saved, 1)

            def last_rows(half):
                t = halves[half]
                dve.wait_ge(last_elu, half * 2 + 2)
                nc.vector.scalar_tensor_tensor(out=ex[:, t, :], in0=ex[:, t, :], scalar=1.0, in1=rl[:, t, :],
                                               op0=ALU.min, op1=ALU.add).then_inc(last_sum, 1)
                dve.wait_ge(last_sum, half + 1)
                if half == 0:
                    dve.wait_ge(xb_in[0], NB * 16)
                    dve.wait_ge(xn_free[0], NB)
                nc.vector.scalar_tensor_tensor(out=xn[:, t, :], in0=ex[:, t, :], scalar=-1.0, in1=xb[:, t, :],
                                               op0=ALU.add, op1=ALU.add).then_inc(last_xn, 1)

            def last_statistics(half):
                dve.wait_ge(last_xn, half + 1)
                for t in range(half * HR, half * HR + HR):
                    ins = nc.vector.bn_stats(bn[:, t, :], xn[:, t, :])
                ins.then_inc(last_parts, 1)
                dve.wait_ge(last_parts, half + 1)
                for t in range(half * HR, half * HR + HR):
                    ins = nc.vector.bn_aggr(mv[:, t, :], bn[:, t, :])
                ins.then_inc(last_stats, 1)
                add_eps(half * HR, HR, last_stats, half + 1).then_inc(last_eps, 1)

            def last_normalise(half):
                dve.wait_ge(last_rstd, half + 1)
                normalise(1, lambda t: xn[:, t, :], 0, half, e * 2 + half)

            last_rows(0)
            last_statistics(0)
            last_rows(1)
            last_normalise(0)
            last_statistics(1)
            last_normalise(1)
            scale_operands(1)

            def layer1_body(ib, cc, early=False, scale=None):
                body = ib * NCC + cc
                for k in range(BODY):
                    if k % CT == 0:
                        dve.wait_ge(mask_in[k // CT], body * 16 + 16)
                    make_p(1, k, ib, cc, body * BODY + k)
                    if k == 2 and scale is not None:
                        scale_g(1, scale)
                    if early and k == 4:
                        save_block(1, ib - 1)
                    if early and k == 6:
                        result(ib - 1)

            with dve.Fori(0, NCC - 1) as cc:
                layer1_body(0, cc, scale=cc + 1)
            layer1_body(0, NCC - 1)
            if NB > 1:
                dve.wait_ge(q_rest[1], 16)
            with dve.Fori(1, NB) as ib:
                layer1_body(ib, 0, early=True)
                with dve.Fori(1, NCC) as cc:
                    layer1_body(ib, cc)
            dve.wait_ge(acc_copied[1], NB * BANKS)
            nc.vector.reciprocal(rec[:, :], hp[:, :, F:GW].rearrange("p t o -> p (t o)")).then_inc(rec_done[1], 1)
            dve.wait_ge(rec_done[1], NB)
            dve.wait_ge(xb_in[1], NB * 16)
            dve.wait_ge(xn_free[1], NB)
            for half, t in enumerate(halves):
                nc.vector.tensor_tensor(hp[:, t, 0:F], hp[:, t, 0:F], rec[:, t].to_broadcast([P, HR, F]), ALU.mult).then_inc(last_saved, 1)
                dve.wait_ge(last_saved, 3 + half)
                nc.vector.tensor_tensor(xn[:, t, :], hp[:, t, 0:F], xb[:, t, :], ALU.add).then_inc(xn_ready[1], 1)

        @block.tensor
        def _(pe):
            pe.sem_inc(transposed, ROW_SLOT_PAIRS)
            for l in L:
                pe.sem_inc(p_used[l], PR)
                pe.sem_inc(ht_pe[l], HID_SLOTS)
                pe.sem_inc(wh_ready[l], 2)
            pe.wait_ge(w_in, 64)
            pe.wait_ge(const_ready, 8)
            for l in L:
                if l:
                    pe.wait_ge(wprep_sb, 2)
                pe.transpose(bank[0][:, 0:P], wa[:, l, 0:F], ident[:, :]).then_inc(wprep_pe, 1)
                pe.wait_ge(wprep_sb, 2 * l + 1)
                pe.matmul(bank[1][:, 0:2], w_T[:, :], a_sb[:, l, :], start=True, stop=True).then_inc(wprep_pe, 1)
            pe.wait_ge(wprep_sb, 4)

            def transpose_half(l, unit, half, banks, ready=None, count=None):
                if ready is None:
                    ready, count = hid_ready[l], unit + 1
                pe.wait_ge(ready, count)
                pe.wait_ge(ht_ready[l], unit + 1)
                for t in range(HR):
                    mm = pe.transpose(bank[banks[0]][:, t * P:(t + 1) * P], hid[:, half, t, :], ident[:, :])
                mm.then_inc(ht_pe[l], 1)

            def project_half(l, unit, half, banks):
                pe.wait_ge(ht_ready[l], unit + 1 + SETS[l])
                pe.wait_ge(wh_copied[l], unit + 1)
                for t in range(HR):
                    o = bank[banks[1 + t // 3]][:, (t % 3) * PW:(t % 3) * PW + PW]
                    mm = pe.matmul(o, hT[:, half, t * P:(t + 1) * P], wa[:, l, :], start=(t % 3 == 0), stop=True, skip_group_check=True)
                mm.then_inc(wh_ready[l], 1)

            def share(l):
                pe.wait_ge(mx_v[l], 1)
                pe.transpose(bank[7][0:1, 0:P], mx[:, 0:1], ident[:, :]).then_inc(mx_pe[l], 1)
                pe.wait_ge(mx_v[l], 2)
                pe.matmul(bank[6][:, 0:1], ones[0:1, :], mx[0:1, 1:2], start=True, stop=True).then_inc(mx_pe[l], 1)
                pe.wait_ge(hs_v[l], 2)
                pe.matmul(bank[2][:, 0:F], hs_rep[:, :], wa[:, l, 0:F], start=True, stop=True).then_inc(mx_pe[l], 1)
                pe.wait_ge(q_v[l], 1)
                pe.transpose(bank[7][0:NT, P:2 * P], qc_sb[:, :], ident[:, :]).then_inc(q_pe[l], 1)
                pe.wait_ge(q_v[l], 2)
                for t in range(BT):
                    mm = pe.matmul(bank[5 + t // HR][:, (t % HR) * P:(t % HR + 1) * P], ident[:, t:t + 1].to_broadcast([P, P]),
                                   qT_sb[:, :], start=(t % HR == 0), stop=True, skip_group_check=True)
                    if t % HR == HR - 1:
                        mm.then_inc(q_row_pe[l], 1)

            def transposes(q, pieces, pair_ahead):
                if q % 2 == 0:
                    pe.wait_ge(converted, pieces + ADJ_SLOTS)
                pe.wait_ge(evacuated, pair_ahead + 1)
                for r in range(BT):
                    mm = pe.transpose(pt[q % 2][:, r * P:(r + 1) * P],
                                      row_sb[:, q // 2, r, (q % 2) * P:(q % 2 + 1) * P], ident16[:, :])
                mm.then_inc(transposed, 1)

            def open_first(k):
                pe.matmul(bank[k][:, 0:PER_BANK * GW], tiny[:, :], mean_v[:, :, :].rearrange("p t w -> p (t w)"),
                          start=True, stop=False, skip_group_check=True)

            def open_accumulators(k):
                pe.matmul(bank[k][:, 0:PER_BANK * GW], tiny16[:, :], mean16[:, :, :].rearrange("p t w -> p (t w)"),
                          start=True, stop=False, skip_group_check=True)

            def products(l, k, cc, step, new_block=None):
                pe.wait_ge(p_ready[l], step + 1 + COL_SLOTS)
                g = g_sb[l][:, bass.ds(cc * BODY + k, 1), 0:GW].rearrange("p t w -> p (t w)")
                for r in range(BT):
                    if new_block is not None and r % PER_BANK == 0:
                        pe.wait_ge(acc_copied[l], new_block * BANKS - BANKS + r // PER_BANK + 1)
                        open_accumulators(r // PER_BANK)
                    mm = pe.matmul(acc_tile(r), p_sb[:, k % PR, r * P:(r + 1) * P], g, start=False, stop=False,
                                   skip_group_check=True)
                    if r % PER_BANK == PER_BANK - 1:
                        mm.then_inc(bank_done[l][r // PER_BANK], 1)
                mm.then_inc(p_used[l], 1)

            with pe.Fori(0, NB // 2) as pair:
                for k in range(4):
                    transpose_half(0, pair * 4 + k, k % 2, PROJECTION_BANKS[k % 2],
                                   *((hid_ready[0], pair * 3 + k + 1) if k < 3 else (hid_ready_s, pair + 1)))
                    if k:
                        project_half(0, pair * 4 + k - 1, (k - 1) % 2, PROJECTION_BANKS[(k - 1) % 2])
                project_half(0, pair * 4 + 3, 1, PROJECTION_BANKS[1])
            for q in range(AHEAD):
                transposes(q, 2, q)
            share(0)

            def layer0_body(ib, cc, early=None, scaled=False):
                body = ib * NCC + cc
                if scaled:
                    pe.wait_ge(g_ready[0], cc + 1)
                for k in range(BODY):
                    if k % CT == 1:
                        for q in (k // 2 + AHEAD, k // 2 + AHEAD + 1):
                            transposes(q % PAIRS, 2 * (2 * body + q // 2) + 2, body * PAIRS + q)
                    products(0, k, cc, body * BODY + k, new_block=ib if early == 0 and k == 0 else None)
                    if early is not None:
                        at, e = early * BODY + k, ib - 1
                        if at == 28 or at == 31:
                            transpose_half(1, e * 2 + (at - 28) // 3, (at - 28) // 3, PROJECTION_BANKS[0])
                        if at == 32 or at == 36:
                            project_half(1, e * 2 + (at - 32) // 4, (at - 32) // 4, PROJECTION_BANKS[0])

            pe.wait_ge(mean_s[0], 1)
            for k in range(BANKS):
                open_first(k)
            pe.wait_ge(f_placed[0], 1)
            with pe.Fori(0, NCC) as cc:
                layer0_body(0, cc, scaled=True)
            pe.wait_ge(mean_p[0], 5)
            with pe.Fori(1, NB) as ib:
                for j in range(EARLY):
                    layer0_body(ib, j, early=j)
                with pe.Fori(EARLY, NCC) as cc:
                    layer0_body(ib, cc)
            e = NB - 1
            for half in range(2):
                transpose_half(1, e * 2 + half, half, PROJECTION_BANKS[0])
                project_half(1, e * 2 + half, half, PROJECTION_BANKS[0])
            share(1)

            def layer1_body(ib, cc, first=False, scaled=False):
                body = ib * NCC + cc
                if scaled:
                    pe.wait_ge(g_ready[1], cc + 1)
                for k in range(BODY):
                    products(1, k, cc, body * BODY + k, new_block=ib if first and k == 0 else None)

            pe.wait_ge(mean_s[1], 1)
            for k in range(BANKS):
                open_first(k)
            pe.wait_ge(f_placed[1], 1)
            with pe.Fori(0, NCC) as cc:
                layer1_body(0, cc, scaled=True)
            pe.wait_ge(mean_p[1], 5)
            with pe.Fori(1, NB) as ib:
                layer1_body(ib, 0, first=True)
                with pe.Fori(1, NCC) as cc:
                    layer1_body(ib, cc)


_INS = ['x', 'adj', 'L0_gnn_W', 'L0_gnn_a', 'L1_gnn_W', 'L1_gnn_a']
_OUTS = [((8192, 128), 'float32')]


def kernel(**inputs):
    import numpy as _np
    import concourse.bacc as _bacc
    from concourse import mybir as _mybir
    from concourse.bass_utils import run_bass_kernel_spmd as _run

    nc = _bacc.Bacc("TRN2", target_bir_lowering=False, num_devices=1)
    arrays, args = {}, []
    for name in _INS:
        a = _np.ascontiguousarray(inputs[name])
        arrays[f"in_{name}_dram"] = a
        args.append(nc.dram_tensor(f"in_{name}_dram", a.shape, _mybir.dt.from_np(a.dtype), kind="ExternalInput").ap())
    for i, (shape, dtype) in enumerate(_OUTS):
        dt = _mybir.dt.from_np(_np.dtype(dtype))
        args.append(nc.dram_tensor(f"out_{i}_dram", shape, dt, kind="ExternalOutput").ap())
    gat_two_layers(nc, *args)
    r = _run(nc, [arrays], core_ids=[0])
    got = tuple(r.results[0][f"out_{i}_dram"] for i in range(len(_OUTS)))
    return got[0]
```
